# Optimizing a Trainium2 kernel written in Bass

```python
import numpy as np
import jax
import jax.numpy as jnp

def _softmax(x, axis=-1):
    return jax.nn.softmax(x, axis=axis)

def _gelu(x):
    return jax.nn.gelu(x, approximate=True)

def _silu(x):
    return jax.nn.silu(x)

def _sigmoid(x):
    return jax.nn.sigmoid(x)

def _layernorm(x, axis=-1, eps=1e-05):
    m = jnp.mean(x, axis=axis, keepdims=True)
    v = jnp.var(x, axis=axis, keepdims=True)
    return (x - m) / jnp.sqrt(v + eps)

def _scatter_add(tgt, idx, src, axis=0):
    return tgt.at[idx].add(src)

def _segment_sum(src, seg, n):
    return jax.ops.segment_sum(src, seg, n)
kernel_name = 'mk_metaformer_d1_conv_nhwc128_r2_eb33c0'

def setup_inputs(seed: int=0):
    np.random.seed(seed)
    _w = jnp.asarray

    def _rec_inputs():
        import jax
        import jax.numpy as jnp
        _gk = jax.random.key(seed)
        x = -0.000125 + 0.9999 * jax.random.normal(jax.random.fold_in(_gk, 1), (1, 256, 256, 64), jnp.float32)
        return x
    x = _rec_inputs()

    def _L0_conv_setup():
        import jax, jax.numpy as jnp
        import numpy as np
        C = 64
        N = 256
        B = 1
        EPS = 1e-05

        def _ln_fp32(x, w, b):
            dt = x.dtype
            xf = x.astype(jnp.float32)
            mu = jnp.mean(xf, axis=-1, keepdims=True)
            var = jnp.var(xf, axis=-1, keepdims=True)
            y = (xf - mu) * jax.lax.rsqrt(var + EPS) * w + b
            return y.astype(dt)
        key = jax.random.key(seed)
        ks = jax.random.split(key, 16)
        s = 1.0 / np.sqrt(C)
        inp = {'act': jax.random.normal(ks[0], (B, N, N, C), jnp.float32), 'mask': jnp.ones((B, N, N), jnp.float32), 'ln_in_w': jnp.ones((C,), jnp.float32), 'ln_in_b': jnp.zeros((C,), jnp.float32), 'left_proj_w': jax.random.normal(ks[1], (C, C), jnp.float32) * s, 'left_proj_b': jnp.zeros((C,), jnp.float32), 'right_proj_w': jax.random.normal(ks[2], (C, C), jnp.float32) * s, 'right_proj_b': jnp.zeros((C,), jnp.float32), 'left_gate_w': jax.random.normal(ks[3], (C, C), jnp.float32) * 0.02, 'left_gate_b': jnp.ones((C,), jnp.float32), 'right_gate_w': jax.random.normal(ks[4], (C, C), jnp.float32) * 0.02, 'right_gate_b': jnp.ones((C,), jnp.float32), 'ln_c_w': jnp.ones((C,), jnp.float32), 'ln_c_b': jnp.zeros((C,), jnp.float32), 'out_proj_w': jax.random.normal(ks[5], (C, C), jnp.float32) * s, 'out_proj_b': jnp.zeros((C,), jnp.float32), 'gating_w': jax.random.normal(ks[6], (C, C), jnp.float32) * 0.02, 'gating_b': jnp.ones((C,), jnp.float32)}
        return inp
    _L0_conv_all = _L0_conv_setup()
    _L0_conv_in = {k: v for k, v in _L0_conv_all.items() if k in ('mask', 'ln_in_w', 'ln_in_b', 'left_proj_w', 'left_proj_b', 'right_proj_w', 'right_proj_b', 'left_gate_w', 'left_gate_b', 'right_gate_w', 'right_gate_b', 'ln_c_w', 'ln_c_b', 'out_proj_w', 'out_proj_b', 'gating_w', 'gating_b')}
    del _L0_conv_all

    def _L0_ffn_setup():
        import jax, jax.numpy as jnp
        import numpy as np
        B, N, D, C, E, K = (8, 4096, 64, 64, 8, 2)
        key = jax.random.key(seed)
        k0, k1, k2 = jax.random.split(key, 3)
        x = jax.random.normal(k0, (B, N, D), dtype=jnp.float32)
        router_w = jax.random.normal(k1, (D, E), dtype=jnp.float32) * 0.05
        router_b = jnp.zeros((E,), dtype=jnp.float32)
        expert_w = jax.random.normal(k2, (E, D, C), dtype=jnp.float32) * (1.0 / np.sqrt(D))
        expert_b = jnp.zeros((E, C), dtype=jnp.float32)
        return {'x': x, 'router_w': router_w, 'router_b': router_b, 'expert_w': expert_w, 'expert_b': expert_b}
    _L0_ffn_all = _L0_ffn_setup()
    _L0_ffn_in = {k: v for k, v in _L0_ffn_all.items() if k in ('router_w', 'router_b', 'expert_w', 'expert_b')}
    del _L0_ffn_all
    return {'x': x, 'L0_conv_mask': _L0_conv_in['mask'], 'L0_conv_ln_in_w': _L0_conv_in['ln_in_w'], 'L0_conv_ln_in_b': _L0_conv_in['ln_in_b'], 'L0_conv_left_proj_w': _L0_conv_in['left_proj_w'], 'L0_conv_left_proj_b': _L0_conv_in['left_proj_b'], 'L0_conv_right_proj_w': _L0_conv_in['right_proj_w'], 'L0_conv_right_proj_b': _L0_conv_in['right_proj_b'], 'L0_conv_left_gate_w': _L0_conv_in['left_gate_w'], 'L0_conv_left_gate_b': _L0_conv_in['left_gate_b'], 'L0_conv_right_gate_w': _L0_conv_in['right_gate_w'], 'L0_conv_right_gate_b': _L0_conv_in['right_gate_b'], 'L0_conv_ln_c_w': _L0_conv_in['ln_c_w'], 'L0_conv_ln_c_b': _L0_conv_in['ln_c_b'], 'L0_conv_out_proj_w': _L0_conv_in['out_proj_w'], 'L0_conv_out_proj_b': _L0_conv_in['out_proj_b'], 'L0_conv_gating_w': _L0_conv_in['gating_w'], 'L0_conv_gating_b': _L0_conv_in['gating_b'], 'L0_ffn_router_w': _L0_ffn_in['router_w'], 'L0_ffn_router_b': _L0_ffn_in['router_b'], 'L0_ffn_expert_w': _L0_ffn_in['expert_w'], 'L0_ffn_expert_b': _L0_ffn_in['expert_b']}

def reference(x, L0_conv_mask, L0_conv_ln_in_w, L0_conv_ln_in_b, L0_conv_left_proj_w, L0_conv_left_proj_b, L0_conv_right_proj_w, L0_conv_right_proj_b, L0_conv_left_gate_w, L0_conv_left_gate_b, L0_conv_right_gate_w, L0_conv_right_gate_b, L0_conv_ln_c_w, L0_conv_ln_c_b, L0_conv_out_proj_w, L0_conv_out_proj_b, L0_conv_gating_w, L0_conv_gating_b, L0_ffn_router_w, L0_ffn_router_b, L0_ffn_expert_w, L0_ffn_expert_b):
    import jax
    import jax.numpy as jnp

    def _L0_conv_ref(act, mask, ln_in_w, ln_in_b, left_proj_w, left_proj_b, right_proj_w, right_proj_b, left_gate_w, left_gate_b, right_gate_w, right_gate_b, ln_c_w, ln_c_b, out_proj_w, out_proj_b, gating_w, gating_b):
        import jax, jax.numpy as jnp
        import numpy as np
        C = 64
        N = 256
        B = 1
        EPS = 1e-05

        def _ln_fp32(x, w, b):
            dt = x.dtype
            xf = x.astype(jnp.float32)
            mu = jnp.mean(xf, axis=-1, keepdims=True)
            var = jnp.var(xf, axis=-1, keepdims=True)
            y = (xf - mu) * jax.lax.rsqrt(var + EPS) * w + b
            return y.astype(dt)
        m = mask[..., None]
        a = _ln_fp32(act, ln_in_w, ln_in_b)
        left = m * (a @ left_proj_w.T + left_proj_b) * jax.nn.sigmoid(a @ left_gate_w.T + left_gate_b)
        right = m * (a @ right_proj_w.T + right_proj_b) * jax.nn.sigmoid(a @ right_gate_w.T + right_gate_b)
        t = jnp.einsum('bikc,bjkc->bijc', left.astype(jnp.float32), right.astype(jnp.float32))
        t = _ln_fp32(t, ln_c_w, ln_c_b).astype(act.dtype)
        out = (t @ out_proj_w.T + out_proj_b) * jax.nn.sigmoid(a @ gating_w.T + gating_b)
        return out

    def _L0_ffn_ref(x, router_w, router_b, expert_w, expert_b):
        import jax, jax.numpy as jnp
        import numpy as np
        B, N, D, C, E, K = (8, 4096, 64, 64, 8, 2)
        router_probs = jax.nn.softmax(x @ router_w + router_b, axis=-1)
        top_p, top_i = jax.lax.top_k(router_probs, K)
        top_p = top_p / jnp.sum(top_p, axis=-1, keepdims=True)
        expert_out = jnp.einsum('bnd,edc->bnec', x, expert_w) + expert_b
        gathered = jnp.take_along_axis(expert_out, top_i[..., None], axis=2)
        return jnp.einsum('bnk,bnkc->bnc', top_p, gathered)

    def _gn(v, G=32, eps=1e-05):
        B_, H_, W_, C_ = v.shape
        g = v.reshape(B_, H_, W_, G, C_ // G)
        m = jnp.mean(g, axis=(1, 2, 4), keepdims=True)
        s = jnp.var(g, axis=(1, 2, 4), keepdims=True)
        return ((g - m) / jnp.sqrt(s + eps)).reshape(v.shape)

    def _ln_c(v, eps=1e-06):
        m = jnp.mean(v, axis=-1, keepdims=True)
        s = jnp.var(v, axis=-1, keepdims=True)
        return (v - m) / jnp.sqrt(s + eps)

    def _ln_t(v, eps=1e-05):
        m = jnp.mean(v, axis=-1, keepdims=True)
        s = jnp.var(v, axis=-1, keepdims=True)
        return (v - m) / jnp.sqrt(s + eps)

    def _to_tokens(v):
        B_, H_, W_, C_ = v.shape
        return v.reshape(B_, H_ * W_, C_)

    def _from_tokens(t, like):
        return t.reshape(like.shape)
    x = x + _L0_conv_ref(_ln_c(x), L0_conv_mask, L0_conv_ln_in_w, L0_conv_ln_in_b, L0_conv_left_proj_w, L0_conv_left_proj_b, L0_conv_right_proj_w, L0_conv_right_proj_b, L0_conv_left_gate_w, L0_conv_left_gate_b, L0_conv_right_gate_w, L0_conv_right_gate_b, L0_conv_ln_c_w, L0_conv_ln_c_b, L0_conv_out_proj_w, L0_conv_out_proj_b, L0_conv_gating_w, L0_conv_gating_b)
    t = _to_tokens(x)
    t = t + _L0_ffn_ref(_ln_t(t), L0_ffn_router_w, L0_ffn_router_b, L0_ffn_expert_w, L0_ffn_expert_b)
    x = _from_tokens(t, x)
    return x

_drawn_inputs = setup_inputs


def setup_inputs(seed=0):
    import zlib

    import numpy as np

    out = dict(_drawn_inputs(seed))
    spreads = {'L0_conv_ln_in_w': (1.0, 0.2),
     'L0_conv_ln_in_b': (0.0, 0.1),
     'L0_conv_left_proj_b': (0.0, 0.1),
     'L0_conv_right_proj_b': (0.0, 0.1),
     'L0_conv_left_gate_b': (1.0, 0.2),
     'L0_conv_right_gate_b': (1.0, 0.2),
     'L0_conv_ln_c_w': (1.0, 0.2),
     'L0_conv_ln_c_b': (0.0, 0.1),
     'L0_conv_out_proj_b': (0.0, 0.1),
     'L0_conv_gating_b': (1.0, 0.2),
     'L0_ffn_router_b': (0.0, 0.1),
     'L0_ffn_expert_b': (0.0, 0.1)}
    factors = {}
    for name, (base, spread) in spreads.items():
        noise = np.random.default_rng([zlib.crc32(name.encode()), seed]).standard_normal(out[name].shape)
        drawn = base * np.exp(spread * noise) if base else spread * noise
        out[name] = jnp.asarray(drawn.astype(out[name].dtype))
    for name, factor in factors.items():
        out[name] = (out[name] * factor).astype(out[name].dtype)
    return out
```

```python
from contextlib import ExitStack

import concourse.bass as bass
from concourse import mybir

F32 = mybir.dt.float32
F32R = mybir.dt.float32r
I32 = mybir.dt.int32
ALU = mybir.AluOpType
ACT = mybir.ActivationFunctionType
AX = mybir.AxisListType

P = 128
N = 256
C = 64
E = 8
Q = 2
ROWS = 16
BLOCKS = N // ROWS
GROUP = 4
GROUPS = ROWS // GROUP
CHUNK = 8
CHUNKS = C // CHUNK
RUN = CHUNK * ROWS
UNIT_J = 8
STEP_J = 2 * UNIT_J
STEPS = 2 * N // STEP_J
JP = UNIT_J // 2
WIDE = JP * P
CYCLE = 6
HEAD = 4
LOOPS = (STEPS - 2 * HEAD) // CYCLE
TAIL = HEAD + LOOPS * CYCLE
TOK = STEP_J
ROUTE = 4 * E
POOL_EXPERTS = (3, 6)
DVE_EXPERTS = tuple(e for e in range(E) if e not in POOL_EXPERTS)
ND, NP_ = len(DVE_EXPERTS), len(POOL_EXPERTS)
NZ = 4
EPS_LN = 1e-5
EPS_OUTER = 1e-6
SEED = float(0x5F3759DF)
BIG = 3e38
PROJ = ["left_proj", "right_proj", "left_gate", "right_gate", "gating", "out_proj"]
LRG = 4 * C
RSTD_OPS = 14
PICK_OPS = 22
STAT_OPS_A = 13
EVEN_USES = [("bcast", 0), ("bcast", 1), ("y", 0)] + [("bcast", e) for e in range(2, E)]
RING_USES = [EVEN_USES, EVEN_USES + [("pack", 0), ("pack", 1)]]


def ring_index(h, kind, e):
    return RING_USES[h].index((kind, e))


def ring_bank(h, kind, e):
    return (h * len(RING_USES[0]) + ring_index(h, kind, e)) % 2


def bcast_bank(h, e):
    return ring_bank(h, "bcast", e)


def y_bank(h):
    return ring_bank(1 - h, "y", 0)


def pack_bank(w):
    return ring_bank(1, "pack", w)


def after(n, k):
    return not isinstance(n, int) or n >= k


def metaformer_kernel(nc, x, mask, weights, router_w, router_b, expert_w, expert_b, out):
    lr_dram = nc.dram_tensor("left_right_scratch", [BLOCKS, P, Q * 2 * C * ROWS], F32, kind="Internal").ap()
    x_rows = x.rearrange("a (b r) (p q) c -> (a b) p r (q c)", r=ROWS, q=Q)
    x_steps = x.rearrange("a (h p) (s j) c -> (a h) s p j c", p=P, j=STEP_J)
    out_steps = out.rearrange("a (h p) (s j) c -> (a h) s p j c", p=P, j=STEP_J)
    HALF = STEPS // 2

    with ExitStack() as ctx:
        def sem(name):
            return ctx.enter_context(nc.semaphore(name))

        def keep(name, shape, dt=F32):
            return ctx.enter_context(nc.sbuf_tensor(name, shape, dt))

        ident = keep("ident", [P, P])
        w_exp = keep("w_exp", [P, E, P])
        w_og = keep("w_og", [P, 2, P])
        w_router = keep("w_router", [P, 2 * E])
        bias_hi = keep("bias_hi", [P, 2, P], F32R)
        bias_lo = keep("bias_lo", [P, 2, P], F32R)
        router_bias = keep("router_bias", [P, E])
        order = keep("order", [P, E])
        rx = keep("rx", [P, 2 * N])
        bx = keep("bx", [P, 2 * N])

        def layer(tensors, psums=()):
            made = []
            with ExitStack() as c:
                for name, shape, *dt in tensors:
                    made.append(c.enter_context(nc.sbuf_tensor(name, shape, *(dt or [F32]))))
                for name, shape in psums:
                    made.append(c.enter_context(nc.psum_tensor(name, shape, F32)))
            return made

        (w_nat, ln_col, bias_row, w_diff, ones, e_nat, r_nat, eb_wide, mask_in) = layer([
            ("w_nat", [C, 6, 2, C]), ("ln_col", [P, 4]), ("bias_row", [1, 6 * C]), ("w_diff", [P, 6 * C]),
            ("ones", [P, P]), ("e_nat", [P, E, C]), ("r_nat", [P, E]), ("eb_wide", [P, 2, P]),
            ("mask_in", [P, 2, N])])
        setup_bytes = 4 * (12 * C + 4 + 6 * C + 6 * C + P + E * C + E + 2 * P + 2 * N)
        (_, w_proj, w_lr, mt, r_all, b_all, xa, xh, xts, sig_a, stage, bst, nv, ny, nt) = layer([
            ("skip_setup", [P, setup_bytes // 4 + 128]),
            ("w_proj", [P, 6 * C]),
            ("w_left_right", [P, Q, LRG]),
            ("mt", [P, N, Q]), ("r_all", [P, N, Q]), ("b_all", [P, N, Q]),
            ("xa", [P, 2, ROWS, Q * C]), ("xh", [P, 2, ROWS, Q * C]), ("xts", [P, 2, GROUP * P]),
            ("sig_a", [P, GROUP, Q, 2 * C]), ("stage", [P, 2, Q, 2 * CHUNKS, ROWS, CHUNK]),
            ("bst", [P, ROWS, 6]), ("nv", [P, ROWS * Q]), ("ny", [P, ROWS * Q]), ("nt", [P, ROWS * Q])])
        (ps_set,) = layer([], [("ps_set", [P, 8, 512])])
        (xt_a, pr_a) = layer([], [("xt_a", [P, 2, 512]), ("pr_a", [P, GROUP, Q * LRG])])

        (t_all, chunk) = layer([("t_all", [P, C, 2 * N]), ("chunk", [P, 2, 2 * Q, BLOCKS, RUN])])
        (ein,) = layer([], [("ein", [P, 4, 512])])

        (_, sel, xc, xn, tn, ttn, xtn, sig_c, x2t, zb, bcs, wt, outc, bst_t, bst_x, v32, y32, t32, rr, bt, lg, lo, l2,
         o1, m1, m2, pm, dd, ws, pk) = layer([
            ("t_keep", [P, C, 2 * N]),
            ("sel", [P, 2, E, P], F32R),
            ("xc", [P, 2, STEP_J, C]), ("xn", [P, 2, UNIT_J, C]), ("tn", [P, 2, UNIT_J, C]),
            ("ttn", [P, WIDE]), ("xtn", [P, WIDE]), ("sig_c", [P, WIDE]), ("x2t", [P, 3, 2, WIDE]),
            ("zb", [P, NZ, WIDE]), ("bcs", [P, 2, WIDE]), ("wt", [P, 2, 2, WIDE // 2], F32R),
            ("outc", [P, 2, UNIT_J, C]), ("bst_t", [P, TOK // 2, 6]), ("bst_x", [P, 2, TOK // 2, 6]),
            ("v32", [P, 2 * TOK]), ("y32", [P, 2 * TOK]), ("t32", [P, 2 * TOK]), ("rr", [P, 2, 2 * TOK]),
            ("bt", [P, 2, TOK]), ("lg", [P, 2, TOK, E]), ("lo", [P, TOK, E]), ("l2", [P, TOK, E]),
            ("o1", [P, TOK, E]), ("m1", [P, TOK]), ("m2", [P, TOK]), ("pm", [P, TOK]),
            ("dd", [P, TOK]), ("ws", [P, 2, TOK]), ("pk", [P, TOK, ROUTE], F32R)])
        (b_t, b_g, b_x, b_d, b_l, b_m, ring) = layer([], [
            ("b_t", [P, 512]), ("b_g", [P, 512]), ("b_x", [P, 512]), ("b_d", [P, 512]), ("b_l", [P, 512]),
            ("b_m", [P, 512]), ("ring", [P, 2, 512])])

        set_step = sem("set_step"); w_in = sem("w_in"); id_made = sem("id_made"); pool_const = sem("pool_const")
        set_pe = sem("set_pe"); set_dve = sem("set_dve"); set_act = sem("set_act")
        x_in = [sem("x_in0"), sem("x_in1")]
        stats_ready = sem("stats_ready"); stat_step = sem("stat_step")
        xh_step = sem("xh_step"); xh_ready = sem("xh_ready")
        xt_ready = sem("xt_ready"); xts_ready = sem("xts_ready"); proj_ready = sem("proj_ready")
        sig_ready = sem("sig_ready"); lr_done = sem("lr_done"); stored = [sem("stored0"), sem("stored1")]
        turn_ready = sem("turn_ready"); turned = sem("turned")
        chunk_in = [sem("chunk_in0"), sem("chunk_in1")]
        ein_ready = sem("ein_ready"); ein_act = sem("ein_act"); ein_dve = sem("ein_dve")
        xc_in = [sem("xc_in0"), sem("xc_in1")]; sel_made = sem("sel_made")
        rstd_step = sem("rstd_step"); rstd_ready = sem("rstd_ready"); bn_t_done = sem("bn_t_done")
        norm_step = sem("norm_step"); norm_ready = sem("norm_ready")
        turns_ready = sem("turns_ready"); turns_out = sem("turns_out"); og_ready = sem("og_ready")
        gate_ready = sem("gate_ready"); om_done = sem("om_done"); x2_ready = sem("x2_ready")
        back_ready = sem("back_ready"); back_done = sem("back_done")
        pick_step = sem("pick_step"); soft_ready = sem("soft_ready")
        pack_turned = sem("pack_turned"); pack_out = sem("pack_out")
        bcast_ready = sem("bcast_ready"); bcast_out = sem("bcast_out")
        z_dve = sem("z_dve"); z_pool = sem("z_pool"); expert_done = sem("expert_done")
        sum_done = sem("sum_done"); y_turned = sem("y_turned"); y_out = sem("y_out")
        out_stored = [sem("out_stored0"), sem("out_stored1")]

        block = ctx.enter_context(nc.Block())
        NW = 40

        @block.sync
        def _(sp):
            for k, name in enumerate(PROJ):
                for half in range(2):
                    sp.dma_start(w_nat[:, k, half, :], weights[name + "_w"]).then_inc(w_in, 16)
                sp.dma_start(bias_row[:, k * C:(k + 1) * C],
                             weights[name + "_b"].rearrange("(a c) -> a c", a=1)).then_inc(w_in, 16)
            for half in range(2):
                part = slice(half * C, half * C + C)
                for col, name in enumerate(["ln_in_w", "ln_c_w"]):
                    sp.dma_start(ln_col[part, 2 * col:2 * col + 1],
                                 weights[name].rearrange("(c a) -> c a", a=1)).then_inc(w_in, 16)
                for col, name in enumerate(["ln_in_b", "ln_c_b"]):
                    sp.dma_start(ln_col[part, 2 * col + 1:2 * col + 2],
                                 weights[name].rearrange("(c a) -> c a", a=1)).then_inc(w_in, 16)
                sp.dma_start(e_nat[part, :, :], expert_w.rearrange("e d c -> d e c")).then_inc(w_in, 16)
                sp.dma_start(r_nat[part, :], router_w).then_inc(w_in, 16)
            sp.dma_start(router_bias[:, :], router_b.rearrange("(a e) -> a e", a=1).broadcast_to([P, E])).then_inc(w_in, 16)
            sp.dma_start(mask_in[:, :, :], mask.rearrange("a (h p) k -> p (a h) k", p=P)).then_inc(w_in, 16)
            sp.wait_ge(pool_const, 3)
            for t in range(4):
                for part in range(2):
                    row = t * ROUTE + (2 + part) * E
                    half = t % 2
                    sp.dma_start(eb_wide[row:row + E, t // 2, half * C:half * C + C], expert_b).then_inc(w_in, 16)

            def load_x(n, b):
                if after(n, 2):
                    sp.wait_ge(xh_ready, n - 1)
                sp.dma_start(xa[:, b, :, :], x_rows[n]).then_inc(x_in[b], 16)

            def block_a(n, b, last=False):
                if not last:
                    load_x(n + 3, 1 - b)
                sp.wait_ge(lr_done, (n + 1) * ROWS)
                sp.dma_start(lr_dram[n], stage[:, b, :, :, :, :].rearrange("p q s r c -> p (q s r c)")).then_inc(stored[b], 16)

            load_x(0, 0)
            load_x(1, 1)
            load_x(2, 0)
            for n in range(BLOCKS):
                block_a(n, n % 2, n + 3 >= BLOCKS)

            for b in range(2):
                sp.wait_ge(stored[b], 16 * BLOCKS // 2)
            sp.wait_ge(turned, 1)

            def load_chunk(c, b):
                if after(c, 2):
                    sp.wait_ge(ein_ready, (c - 1) * CHUNK)
                for u in range(2 * Q):
                    part = lr_dram.rearrange("n p (u c) -> u p n c", u=2 * Q)[u, :, :, c * RUN:(c + 1) * RUN]
                    sp.dma_start(chunk[:, b, u, :, :], part).then_inc(chunk_in[b], 16)

            for c in range(CHUNKS):
                load_chunk(c, c % 2)
            sp.wait_ge(ein_ready, C)

            def load_step(s, b):
                if after(s, 2):
                    sp.wait_ge(turns_ready, s * 2 - 2)
                sp.dma_start(xc[:, b, :, :], x_steps[s // HALF, s % HALF]).then_inc(xc_in[b], 16)

            def store_unit(u, s, h):
                sp.wait_ge(y_out, u + 1)
                sp.dma_start(out_steps[s // HALF, s % HALF][:, h * UNIT_J:h * UNIT_J + UNIT_J, :], outc[:, h, :, :])\
                  .then_inc(out_stored[h], 16)

            def step_c(s, k):
                if not isinstance(s, int) or s + 3 < STEPS:
                    load_step(s + 3, (k + 3) % 2)
                for h in range(2):
                    store_unit(s * 2 + h, s, h)

            load_step(0, 0)
            load_step(1, 1)
            load_step(2, 0)
            for s in range(HEAD):
                step_c(s, s)
            with sp.Fori(0, LOOPS) as i:
                for k in range(HEAD, HEAD + CYCLE):
                    step_c(i * CYCLE + k, k)
            for s in range(TAIL, STEPS):
                step_c(s, s)
            for h in range(2):
                sp.wait_ge(out_stored[h], 16 * STEPS)

        @block.gpsimd
        def _(pool):
            pool.memset(ident[:, :], 0.0).then_inc(id_made, 1)
            pool.memset(ones[:, :], 1.0 / C).then_inc(pool_const, 1)
            pool.memset(w_router[:, :], 0.0).then_inc(pool_const, 1)
            pool.memset(eb_wide[:, :, :], 0.0).then_inc(pool_const, 1)
            pool.memset(w_exp[:, :, :], 0.0).then_inc(pool_const, 1)
            pool.memset(w_og[:, :, :], 0.0).then_inc(pool_const, 1)
            pool.memset(w_lr[:, :, :], 0.0).then_inc(pool_const, 1)
            for e in range(E):
                m = pool.memset(order[:, e:e + 1], float(E - e))
            m.then_inc(pool_const, 1)
            pool.wait_ge(id_made, 1)
            pool.affine_select(out=ident[:, :], in_=ident[:, :], compare_op=ALU.not_equal, fill=1.0, base=0,
                               pattern=[[-1, P]], channel_multiplier=1).then_inc(id_made, 1)

            def block_a(n, b):
                rows = bass.ts(n, ROWS)
                src = xa[:, b, :, :].rearrange("p r (q c) -> p (r q) c", q=Q)
                dst = xh[:, b, :, :].rearrange("p r (q c) -> p (r q) c", q=Q)
                r = r_all[:, rows, :].rearrange("p r q -> p (r q)").unsqueeze(2).broadcast_to([P, ROWS * Q, C])
                m = b_all[:, rows, :].rearrange("p r q -> p (r q)").unsqueeze(2).broadcast_to([P, ROWS * Q, C])
                pool.wait_ge(stats_ready, n + 1)
                if after(n, 2):
                    pool.wait_ge(xt_ready, (n - 1) * GROUPS)
                pool.tensor_tensor(dst, src, r, ALU.mult).then_inc(xh_step, 1)
                pool.wait_ge(xh_step, n + 1)
                pool.tensor_tensor(dst, dst, m, ALU.add).then_inc(xh_ready, 1)

            block_a(0, 0)
            block_a(1, 1)
            with pool.Fori(1, BLOCKS // 2) as i:
                block_a(i * 2, 0)
                block_a(i * 2 + 1, 1)

            def front(v, s, k, h):
                b = v % 2 if isinstance(v, int) else h
                cols = slice(h * UNIT_J, h * UNIT_J + UNIT_J)
                pool.wait_ge(xc_in[k % 2], s // 2 * 16 + 16 if isinstance(s, int) else (s - k % 2) * 8 + 16)
                pool.wait_ge(rstd_ready, s + 1)
                if after(v, 2):
                    pool.wait_ge(turns_ready, v - 1)
                t_in = t_all[:, :, bass.ts(v, UNIT_J)].rearrange("p c j -> p j c")
                r_t = rr[:, k % 2, TOK + h * UNIT_J:TOK + (h + 1) * UNIT_J].unsqueeze(2).broadcast_to([P, UNIT_J, C])
                b_tt = bt[:, k % 2, cols].unsqueeze(2).broadcast_to([P, UNIT_J, C])
                r_x = rx[:, bass.ts(v, UNIT_J)].unsqueeze(2).broadcast_to([P, UNIT_J, C])
                b_xx = bx[:, bass.ts(v, UNIT_J)].unsqueeze(2).broadcast_to([P, UNIT_J, C])
                pool.tensor_tensor(tn[:, h, :, :], t_in, r_t, ALU.mult).then_inc(norm_step, 1)
                pool.tensor_tensor(xn[:, h, :, :], xc[:, k % 2, cols, :], r_x, ALU.mult).then_inc(norm_step, 1)
                pool.wait_ge(norm_step, v * 2 + 1)
                pool.tensor_tensor(tn[:, h, :, :], tn[:, h, :, :], b_tt, ALU.add)
                pool.wait_ge(norm_step, v * 2 + 2)
                pool.tensor_tensor(xn[:, h, :, :], xn[:, h, :, :], b_xx, ALU.add).then_inc(norm_ready, 1)

            def scale(e, u, k, h):
                i = POOL_EXPERTS.index(e)
                pool.wait_ge(bcast_out, u * NP_ + i + 1)
                if after(u, 1) or e >= NZ:
                    pool.wait_ge(expert_done, u * E + e - NZ + 1)
                pool.tensor_tensor(zb[:, e % NZ, :], bcs[:, i % 2, :], x2t[:, k % 3, h, :], ALU.mult).then_inc(z_pool, 1)

            def step_c(s, k, ahead=True, experts=True):
                for h in range(2):
                    if ahead:
                        front(s * 2 + h + 4, s + 2, k + 2, h)
                    if experts:
                        for e in POOL_EXPERTS:
                            scale(e, s * 2 + h, k, h)

            pool.wait_ge(ein_ready, (CHUNKS - 1) * CHUNK)
            kinds = ident[:, :].rearrange("p (t k e) -> p t k e", t=4, k=4)
            for t in range(4):
                ins = pool.tensor_tensor(sel[:, t // 2, :, t % 2 * C:(t % 2 + 1) * C],
                                         kinds[:, t, 0, :].unsqueeze(2).broadcast_to([P, E, C]),
                                         kinds[:, t, 1, :].unsqueeze(2).broadcast_to([P, E, C]), ALU.add)
            ins.then_inc(sel_made, 1)
            pool.wait_ge(ein_ready, C)
            step_c(-2, -2, experts=False)
            step_c(-1, -1, experts=False)
            for s in range(HEAD):
                step_c(s, s)
            with pool.Fori(0, LOOPS) as i:
                for k in range(HEAD, HEAD + CYCLE):
                    step_c(i * CYCLE + k, k)
            for s in range(TAIL, STEPS):
                step_c(s, s, ahead=s + 2 < STEPS)

        @block.scalar
        def _(act):
            act.wait_ge(set_pe, 2)
            for h in range(2):
                for q in range(Q):
                    ins = act.activation(mt[:, h * P:h * P + P, q], ps_set[:, 1, (2 * h + q) * P:(2 * h + q + 1) * P], ACT.Copy)
            ins.then_inc(set_act, 1)

            def evacuate(n, g, b):
                act.wait_ge(xt_ready, n * GROUPS + g + 1)
                if after(n, 1) or g >= 2:
                    act.wait_ge(proj_ready, (n * GROUPS + g - 1) * GROUP)
                act.activation(xts[:, g % 2, :], xt_a[:, g % 2, :], ACT.Copy).then_inc(xts_ready, 1)

            def gates(n, g):
                for r in range(GROUP):
                    act.wait_ge(proj_ready, (n * GROUPS + g) * GROUP + r + 1)
                    act.activation(sig_a[:, r, :, :], pr_a[:, r, :].rearrange("p (q c) -> p q c", q=Q)[:, :, 2 * C:4 * C],
                                   ACT.Sigmoid).then_inc(sig_ready, 1)

            def block_a(n, b, last=False):
                for g in range(GROUPS):
                    if g < GROUPS - 1:
                        evacuate(n, g + 1, b)
                    elif not last:
                        evacuate(n + 1, 0, b)
                    gates(n, g)

            evacuate(0, 0, 0)
            block_a(0, 0)
            block_a(1, 1)
            with act.Fori(1, BLOCKS // 2 - 1) as i:
                block_a(i * 2, 0)
                block_a(i * 2 + 1, 1)
            block_a(BLOCKS - 2, 0)
            block_a(BLOCKS - 1, 1, True)
            act.wait_ge(turn_ready, 1)
            for k, dst in enumerate([rx, bx]):
                for h in range(2):
                    for q in range(Q):
                        ins = act.activation(dst[:, h * N:h * N + N].rearrange("p (j q) -> p j q", q=Q)[:, :, q],
                                             pr_a[:, k, (2 * h + q) * P:(2 * h + q + 1) * P], ACT.Copy)
            ins.then_inc(turned, 1)

            def chunk_b(c):
                for k in range(0, CHUNK, 2):
                    act.wait_ge(ein_ready, c * CHUNK + k + 1)
                    act.activation(t_all[:, bass.ds(c * CHUNK + k, 1), :].rearrange("p a n -> p (a n)"),
                                   ein[:, k % 4, :], ACT.Copy).then_inc(ein_act, 1)

            with act.Fori(0, CHUNKS) as c:
                chunk_b(c)

            def front(v):
                act.wait_ge(turns_ready, v + 1)
                if after(v, 1):
                    act.wait_ge(og_ready, v)
                act.activation(ttn[:, :], b_t[:, :], ACT.Copy)
                act.activation(xtn[:, :], b_g[:, :], ACT.Copy).then_inc(turns_out, 1)

            def gate(v):
                act.wait_ge(og_ready, v + 1)
                if after(v, 1):
                    act.wait_ge(x2_ready, v)
                act.activation(sig_c[:, :], b_g[:, :], ACT.Sigmoid).then_inc(gate_ready, 1)

            def y_evacuate(u, h):
                act.wait_ge(y_turned, u + 1)
                if after(u, 2):
                    act.wait_ge(out_stored[h], (u - h) * 8 if not isinstance(u, int) else u // 2 * 16)
                act.activation(outc[:, h, :, :].rearrange("p j c -> p (j c)"), ring[:, y_bank(h), :], ACT.Copy)\
                   .then_inc(y_out, 1)

            def bcast(e, u, h):
                i = POOL_EXPERTS.index(e)
                act.wait_ge(bcast_ready, u * E + e + 1)
                if after(u, 1):
                    act.wait_ge(z_pool, (u - 1) * NP_ + i + 1)
                act.activation(bcs[:, i % 2, :], ring[:, bcast_bank(h, e), :], ACT.Copy).then_inc(bcast_out, 1)

            def soft(s):
                act.wait_ge(pick_step, (s + 1) * PICK_OPS + 14)
                act.activation(ws[:, 0, :], dd[:, :], ACT.Sigmoid)
                act.activation(ws[:, 1, :], dd[:, :], ACT.Sigmoid, scale=-1.0).then_inc(soft_ready, 1)

            def pack(w, k, h):
                act.wait_ge(pack_turned, w + 1)
                act.activation(wt[:, k % 2, h, :], ring[:, pack_bank(h), 0:WIDE // 2], ACT.Copy).then_inc(pack_out, 1)

            def step_c(s, k, ahead=True, route=True, experts=True):
                for h in range(2):
                    u = s * 2 + h
                    if ahead:
                        front(u + 4)
                    if experts and after(u, 1):
                        y_evacuate(u - 1, 1 - h)
                    if ahead:
                        gate(u + 4)
                    if experts:
                        bcast(POOL_EXPERTS[0], u, h)
                    if route and h == 1:
                        soft(s)
                    if experts:
                        bcast(POOL_EXPERTS[1], u, h)
                    if route and h == 1:
                        for w in range(2):
                            pack(s * 2 + 2 + w, k + 1, w)

            step_c(-2, -2, route=False, experts=False)
            step_c(-1, -1, experts=False)
            for s in range(HEAD):
                step_c(s, s)
            with act.Fori(0, LOOPS) as i:
                for k in range(HEAD, HEAD + CYCLE):
                    step_c(i * CYCLE + k, k)
            for s in range(TAIL, STEPS):
                step_c(s, s, ahead=s + 2 < STEPS, route=s + 1 < STEPS)
            y_evacuate(2 * STEPS - 1, 1)

        @block.tensor
        def _(pe):
            pe.wait_ge(id_made, 2)
            pe.wait_ge(w_in, 16 * NW)
            for k in range(6):
                m = pe.transpose(ps_set[:, 0, k * C:(k + 1) * C], w_nat[:, k, :, :].rearrange("p a c -> p (a c)"), ident[0:C, 0:C])
            m.then_inc(set_pe, 1)
            for h in range(2):
                for q in range(Q):
                    m = pe.transpose(ps_set[:, 1, (2 * h + q) * P:(2 * h + q + 1) * P],
                                     mask_in[:, h, :].rearrange("p (k q) -> p k q", q=Q)[:, :, q], ident[:, :])
            m.then_inc(set_pe, 1)
            pe.matmul(ps_set[:, 2, :], ones[0:C, :], e_nat[0:C, :, :].rearrange("p e c -> p (e c)"), start=True, stop=True)
            pe.matmul(ps_set[:, 3, 0:E], ones[0:C, :], r_nat[0:C, :], start=True, stop=True).then_inc(set_pe, 1)
            pe.wait_ge(set_dve, 1)
            pe.matmul(ps_set[:, 4, 0:6 * C], ones[0:C, :], w_diff[0:C, :], start=True, stop=False)
            pe.matmul(ps_set[:, 4, 0:6 * C], ones[0:1, :], bias_row[:, :], start=False, stop=True).then_inc(set_pe, 1)
            pe.wait_ge(set_dve, 3)
            pe.wait_ge(set_act, 1)

            def turn(n, g, b):
                pe.wait_ge(xh_ready, n + 1)
                if after(n, 1) or g >= 2:
                    pe.wait_ge(xts_ready, n * GROUPS + g - 1)
                for r in range(GROUP):
                    m = pe.transpose(xt_a[:, g % 2, r * P:(r + 1) * P], xh[:, b, g * GROUP + r, :], ident[:, :])
                m.then_inc(xt_ready, 1)

            def project(n, g):
                pe.wait_ge(xts_ready, n * GROUPS + g + 1)
                for r in range(GROUP):
                    if after(n, 1) or g >= 1:
                        pe.wait_ge(lr_done, (n * GROUPS + g - 1) * GROUP + r + 1)
                    pe.matmul(pr_a[:, r, :], xts[:, g % 2, r * P:(r + 1) * P], w_lr[:, :, :].rearrange("p q c -> p (q c)"),
                              start=True, stop=True).then_inc(proj_ready, 1)

            def block_a(n, b, last=False):
                for g in range(GROUPS):
                    if g < GROUPS - 1:
                        turn(n, g + 1, b)
                    elif not last:
                        turn(n + 1, 0, 1 - b)
                    project(n, g)

            turn(0, 0, 0)
            block_a(0, 0)
            block_a(1, 1)
            with pe.Fori(1, BLOCKS // 2 - 1) as i:
                block_a(i * 2, 0)
                block_a(i * 2 + 1, 1)
            block_a(BLOCKS - 2, 0)
            block_a(BLOCKS - 1, 1, True)
            pe.wait_ge(lr_done, BLOCKS * ROWS)
            for k, src in enumerate([r_all, b_all]):
                for h in range(2):
                    for q in range(Q):
                        m = pe.transpose(pr_a[:, k, (2 * h + q) * P:(2 * h + q + 1) * P],
                                         src[:, h * P:h * P + P, q], ident[:, :])
            m.then_inc(turn_ready, 1)
            pe.wait_ge(turned, 1)

            def chunk_b(c, b):
                pe.wait_ge(chunk_in[b], (c // 2 + 1) * 64 if isinstance(c, int) else (c - b) * 32 + 64)
                for k in range(CHUNK):
                    if after(c, 1) or k >= 4:
                        pe.wait_ge(ein_dve if k % 2 else ein_act, c * (CHUNK // 2) + k // 2 - 1)
                    side = chunk[:, b, :, :, :].rearrange("p u n (r c) -> p u (n r) c", c=CHUNK)[:, :, :, k]
                    for h in range(2):
                        for q in range(Q):
                            m = pe.matmul(ein[:, k % 4, h * N:h * N + N],
                                          side[:, 2 * q, h * P:h * P + P], side[:, 2 * q + 1, :], start=q == 0, stop=q == 1)
                    m.then_inc(ein_ready, 1)

            chunk_b(0, 0)
            chunk_b(1, 1)
            with pe.Fori(1, CHUNKS // 2) as i:
                chunk_b(i * 2, 0)
                chunk_b(i * 2 + 1, 1)
            pe.wait_ge(ein_act, C // 2)
            pe.wait_ge(ein_dve, C // 2)

            pe.wait_ge(sel_made, 1)

            pairs = [slice(j * P, j * P + P) for j in range(JP)]
            of_pair = lambda bank, a: bank.rearrange("p (q a i) -> p q a i", q=2, a=2)[:, :, a, :]

            def turns(v, k, h):
                pe.wait_ge(norm_ready, v + 1)
                if after(v, 1):
                    pe.wait_ge(x2_ready, v)
                for dst, src in ((b_t, tn[:, h, :, :]), (b_g, xn[:, h, :, :]),
                                 (b_x, xc[:, k % 2, h * UNIT_J:(h + 1) * UNIT_J, :])):
                    for j in range(JP):
                        m = pe.transpose(dst[:, pairs[j]], src[:, 2 * j:2 * j + 2, :].rearrange("p j c -> p (j c)"), ident[:, :])
                m.then_inc(turns_ready, 1)

            def out_gate(v):
                pe.wait_ge(turns_out, v + 1)
                pe.matmul(b_g[:, :], w_og[:, 0, :], xtn[:, :], start=True, stop=True)
                pe.matmul(b_t[:, :], w_og[:, 1, :], ttn[:, :], start=True, stop=True).then_inc(og_ready, 1)

            def back(v, k, h):
                pe.wait_ge(x2_ready, v + 1)
                if after(v, 1):
                    pe.wait_ge(back_done, v)
                for j in range(JP):
                    pe.transpose(b_d[:, pairs[j]], x2t[:, k % 3, h, pairs[j]], ident[:, :])
                for j in range(JP):
                    m = pe.matmul(b_l[:, j * 2 * E:(j + 1) * 2 * E], x2t[:, k % 3, h, pairs[j]], w_router[:, :],
                                  start=True, stop=True)
                m.then_inc(back_ready, 1)

            def ring_free(h, r, u):
                prev_h, prev_r, w = h, r - 2, u
                if prev_r < 0:
                    prev_h, w = 1 - h, u - 1
                    prev_r += len(RING_USES[prev_h])
                if isinstance(w, int) and w < 0 and RING_USES[prev_h][prev_r][0] != "pack":
                    return
                kind, e = RING_USES[prev_h][prev_r]
                if kind == "bcast" and e in DVE_EXPERTS:
                    pe.wait_ge(z_dve, w * ND + DVE_EXPERTS.index(e) + 1)
                elif kind == "bcast":
                    pe.wait_ge(bcast_out, w * NP_ + POOL_EXPERTS.index(e) + 1)
                elif kind == "y":
                    if after(w, 1):
                        pe.wait_ge(y_out, w)
                else:
                    pe.wait_ge(pack_out, w + 1 + 1 + e)

            def bcast(e, u, k, h):
                ring_free(h, ring_index(h, "bcast", e), u)
                if e == 0:
                    pe.wait_ge(pack_out, u + 1)
                for a in range(2):
                    m = pe.matmul(of_pair(ring[:, bcast_bank(h, e), :], a), sel[:, a, e, :], wt[:, k % 2, h, :],
                                  start=True, stop=True)
                m.then_inc(bcast_ready, 1)

            def bias(u, k, h):
                if after(u, 1):
                    pe.wait_ge(sum_done, u)
                for a in range(2):
                    pe.matmul(of_pair(b_m[:, :], a), bias_hi[:, a, :], wt[:, k % 2, h, :], start=a == 0, stop=False,
                              skip_group_check=True)
                    pe.matmul(of_pair(b_m[:, :], a), bias_lo[:, a, :], wt[:, k % 2, h, :], start=False, stop=False,
                              skip_group_check=True)

            def expert(e, u):
                if e in DVE_EXPERTS:
                    pe.wait_ge(z_dve, u * ND + DVE_EXPERTS.index(e) + 1)
                else:
                    pe.wait_ge(z_pool, u * NP_ + POOL_EXPERTS.index(e) + 1)
                pe.matmul(b_m[:, :], w_exp[:, e, :], zb[:, e % NZ, :], start=False, stop=e == E - 1,
                          skip_group_check=True).then_inc(expert_done, 1)

            def y_turn(u, k, h, slot):
                if slot is not None:
                    ring_free(slot, ring_index(slot, "y", 0), u + 1)
                pe.wait_ge(sum_done, u + 1)
                for j in range(JP):
                    m = pe.transpose(ring[:, y_bank(h), pairs[j]], x2t[:, k % 3, h, pairs[j]], ident[:, :])
                m.then_inc(y_turned, 1)

            def pack(s, w):
                u = s * 2 + 1
                ring_free(1, ring_index(1, "pack", w), u)
                pe.wait_ge(pick_step, (s + 1) * PICK_OPS + PICK_OPS)
                for q in range(2):
                    t0 = w * UNIT_J + 4 * q
                    m = pe.transpose(ring[:, pack_bank(w), pairs[q]],
                                     pk[:, t0:t0 + 4, :].bitcast(F32).rearrange("p j c -> p (j c)"), ident[:, :])
                m.then_inc(pack_turned, 1)

            def step_c(s, k, ahead=True, route=True, experts=True):
                for h in range(2):
                    u = s * 2 + h
                    v = u + 4
                    if experts:
                        bcast(0, u, k, h)
                        bcast(1, u, k, h)
                    if ahead:
                        turns(v, k + 2, h)
                    if experts:
                        bias(u, k, h)
                        expert(0, u)
                        if after(u, 1):
                            y_turn(u - 1, k if h else k - 1, 1 - h, h)
                        bcast(2, u, k, h)
                        expert(1, u)
                    if ahead:
                        out_gate(v)
                    if experts:
                        bcast(3, u, k, h)
                        expert(2, u)
                        bcast(4, u, k, h)
                        expert(3, u)
                    if ahead:
                        back(v, k + 2, h)
                    if experts:
                        bcast(5, u, k, h)
                        expert(4, u)
                        bcast(6, u, k, h)
                        expert(5, u)
                        bcast(7, u, k, h)
                    if route and h == 1:
                        pack(s, 0)
                    if experts:
                        expert(6, u)
                    if route and h == 1:
                        pack(s, 1)
                    if experts:
                        expert(7, u)

            step_c(-2, -2, route=False, experts=False)
            step_c(-1, -1, experts=False)
            for s in range(HEAD):
                step_c(s, s)
            with pe.Fori(0, LOOPS) as i:
                for k in range(HEAD, HEAD + CYCLE):
                    step_c(i * CYCLE + k, k)
            for s in range(TAIL, STEPS):
                step_c(s, s, ahead=s + 2 < STEPS, route=s + 1 < STEPS)
            y_turn(2 * STEPS - 1, STEPS - 1, 1, None)

        @block.vector
        def _(dve):
            in5, out1 = slice(0, 5 * C), slice(5 * C, 6 * C)
            dve.wait_ge(set_pe, 1)
            dve.tensor_scalar(w_proj[:, in5], ps_set[:, 0, in5], ln_col[:, 0:1], None, ALU.mult)
            dve.tensor_scalar(w_proj[:, out1], ps_set[:, 0, out1], ln_col[:, 2:3], None, ALU.mult).then_inc(set_step, 1)
            dve.wait_ge(set_step, 1)
            dve.scalar_tensor_tensor(w_diff[:, in5], ps_set[:, 0, in5], ln_col[:, 1:2], w_proj[:, in5], ALU.mult, ALU.subtract)
            dve.scalar_tensor_tensor(w_diff[:, out1], ps_set[:, 0, out1], ln_col[:, 3:4], w_proj[:, out1], ALU.mult, ALU.subtract)\
               .then_inc(set_dve, 1)
            dve.wait_ge(set_pe, 3)
            dve.wait_ge(pool_const, 7)
            for half in range(2):
                part = slice(half * C, half * C + C)
                dve.tensor_tensor(w_exp[part, :, part], e_nat[part, :, :],
                                  ps_set[part, 2, :].rearrange("p (e c) -> p e c", e=E), ALU.subtract)
                dve.tensor_tensor(w_router[part, half * E:half * E + E], r_nat[part, :], ps_set[part, 3, 0:E], ALU.subtract)
            dve.tensor_copy(bias_hi[:, :, :], eb_wide[:, :, :]).then_inc(set_step, 1)
            dve.wait_ge(set_step, 2)
            dve.tensor_tensor(bias_lo[:, :, :], eb_wide[:, :, :], bias_hi[:, :, :].bitcast(F32), ALU.subtract)
            dve.wait_ge(set_pe, 4)
            dve.tensor_tensor(w_proj[:, :], w_proj[:, :], ps_set[:, 4, 0:6 * C], ALU.add).then_inc(set_dve, 1)
            dve.wait_ge(set_dve, 2)
            for w in range(2):
                for half in range(2):
                    part = slice(half * C, half * C + C)
                    dve.tensor_copy(w_og[part, w, part], w_proj[part, (4 + w) * C:(5 + w) * C])
            for half in range(2):
                part = slice(half * C, half * C + C)
                ins = dve.tensor_copy(w_lr[part, half, :], w_proj[part, 0:LRG])
            ins.then_inc(set_dve, 1)
            dve.wait_ge(set_act, 1)

            stat_a = bst[:, :, :].rearrange("p r (q z) -> p r q z", q=Q)
            wide = lambda ap: ap[:, :].rearrange("p (r q) -> p r q", q=Q)
            by_chunk = lambda ap: ap.rearrange("p (s c) -> p s c", c=CHUNK)

            def bn(n, b, rows):
                for r in rows:
                    ins = dve.bn_stats(bst[:, r, :], xa[:, b, r, :].rearrange("p (q c) -> p c q", q=Q))
                if rows[-1] == ROWS - 1:
                    ins.then_inc(stat_step, 1)

            def rstd_a(n, ks):
                r_out = r_all[:, bass.ts(n, ROWS), :]
                for k in ks:
                    dve.wait_ge(stat_step, n * STAT_OPS_A + 1 + k)
                    if k == 0:
                        ins = dve.tensor_scalar(wide(nv), stat_a[:, :, :, 2], (1 + EPS_LN) / C, EPS_LN * EPS_OUTER,
                                                ALU.mult, ALU.add)
                    elif k == 1:
                        ins = dve.tensor_scalar(ny[:, :].bitcast(I32), nv[:, :].bitcast(I32), -0.5, SEED, ALU.mult, ALU.add)
                    elif k == 10:
                        ins = dve.scalar_tensor_tensor(r_out, wide(nt), 1.5, wide(ny), ALU.add, ALU.mult)
                    elif k == 11:
                        ins = dve.scalar_tensor_tensor(wide(nt), stat_a[:, :, :, 1], -1.0, r_out, ALU.mult, ALU.mult)
                    elif k == 12:
                        ins = dve.tensor_scalar(b_all[:, bass.ts(n, ROWS), :], wide(nt), 1.0, None, ALU.add)
                    elif k % 3 == 2:
                        ins = dve.tensor_tensor(nt[:, :], ny[:, :], ny[:, :], ALU.mult)
                    elif k % 3 == 0:
                        ins = dve.scalar_tensor_tensor(nt[:, :], nt[:, :], -0.5, nv[:, :], ALU.mult, ALU.mult)
                    else:
                        ins = dve.scalar_tensor_tensor(ny[:, :], nt[:, :], 1.5, ny[:, :], ALU.add, ALU.mult)
                    ins.then_inc(stats_ready if k == 12 else stat_step, 1)

            def wait_x(n, b):
                dve.wait_ge(x_in[b], n // 2 * 16 + 16 if isinstance(n, int) else (n - b) * 8 + 16)

            def left_right(n, row, b):
                dve.wait_ge(sig_ready, n * ROWS + row + 1)
                if row == 0 and after(n, 2):
                    dve.wait_ge(stored[b], n // 2 * 16 if isinstance(n, int) else (n - b) * 8)
                for q in range(Q):
                    ins = dve.scalar_tensor_tensor(
                        stage[:, b, q, :, row, :], by_chunk(pr_a[:, row % GROUP, q * LRG:q * LRG + 2 * C]),
                        mt[:, bass.ds(n * ROWS + row, 1), q], by_chunk(sig_a[:, row % GROUP, q, :]), ALU.mult, ALU.mult)
                ins.then_inc(lr_done, 1)

            def block_a(n, b, ahead=True):
                if ahead:
                    wait_x(n + 2, b)
                for row in range(ROWS):
                    if ahead and row < ROWS // 2:
                        bn(n + 2, b, (2 * row, 2 * row + 1))
                    elif ahead:
                        rstd_a(n + 2, ((0, 1), (2, 3), (4, 5), (6, 7), (8, 9), (10,), (11,), (12,))[row - ROWS // 2])
                    left_right(n, row, b)

            for n in range(2):
                wait_x(n, n)
                bn(n, n, range(ROWS))
                rstd_a(n, range(13))
            block_a(0, 0)
            block_a(1, 1)
            with dve.Fori(1, BLOCKS // 2 - 1) as i:
                block_a(i * 2, 0)
                block_a(i * 2 + 1, 1)
            block_a(BLOCKS - 2, 0, False)
            block_a(BLOCKS - 1, 1, False)

            with dve.Fori(0, CHUNKS) as c:
                for k in range(1, CHUNK, 2):
                    dve.wait_ge(ein_ready, c * CHUNK + k + 1)
                    dve.tensor_copy(t_all[:, bass.ds(c * CHUNK + k, 1), :].rearrange("p a n -> p (a n)"), ein[:, k % 4, :])\
                       .then_inc(ein_dve, 1)
            dve.wait_ge(ein_act, C // 2)
            dve.wait_ge(ein_dve, C // 2)

            def stats_t(s, js):
                for j in js:
                    ins = dve.bn_stats(bst_t[:, j, :], t_all[:, :, bass.ds(s * STEP_J + 2 * j, 2)])
                if js[-1] == TOK // 2 - 1:
                    ins.then_inc(bn_t_done, 1)

            def rstd_c(s, k3, ks):
                b = k3 % 2
                t_stat = bst_t[:, :, :].rearrange("p j (t z) -> p j t z", t=2)
                x_stat = bst_x[:, b, :, :].rearrange("p j (t z) -> p j t z", t=2)
                pair = lambda ap: ap.rearrange("p (j t) -> p j t", t=2)
                for k in ks:
                    if k == 0:
                        if after(s, -1):
                            dve.wait_ge(back_done, s * 2 + 4)
                            dve.wait_ge(norm_ready, s * 2 + 4)
                            ins = dve.tensor_scalar(pair(v32[:, 0:TOK]), x_stat[:, :, :, 2], 1.0 / C, EPS_LN, ALU.mult, ALU.add)
                        else:
                            ins = dve.memset(v32[:, 0:TOK], 1.0)
                    elif k == 1:
                        if not isinstance(s, int) or s + 3 < STEPS:
                            dve.wait_ge(bn_t_done, s + 4)
                        ins = dve.tensor_scalar(pair(v32[:, TOK:2 * TOK]), t_stat[:, :, :, 2], 1.0 / C, EPS_LN, ALU.mult, ALU.add)
                    else:
                        dve.wait_ge(rstd_step, (s + 3) * (RSTD_OPS - 1) + k)
                        if k == 2:
                            ins = dve.tensor_scalar(y32[:, :].bitcast(I32), v32[:, :].bitcast(I32), -0.5, SEED, ALU.mult, ALU.add)
                        elif k == 11:
                            ins = dve.scalar_tensor_tensor(rr[:, b, :], t32[:, :], 1.5, y32[:, :], ALU.add, ALU.mult)
                        elif k == 12:
                            ins = dve.scalar_tensor_tensor(pair(t32[:, 0:TOK]), t_stat[:, :, :, 1], -1.0,
                                                           pair(rr[:, b, TOK:2 * TOK]), ALU.mult, ALU.mult)
                        elif k == 13:
                            ins = dve.tensor_scalar(bt[:, b, :], t32[:, 0:TOK], 1.0, None, ALU.add)
                        elif k % 3 == 0:
                            ins = dve.tensor_tensor(t32[:, :], y32[:, :], y32[:, :], ALU.mult)
                        elif k % 3 == 1:
                            ins = dve.scalar_tensor_tensor(t32[:, :], t32[:, :], -0.5, v32[:, :], ALU.mult, ALU.mult)
                        else:
                            ins = dve.scalar_tensor_tensor(y32[:, :], t32[:, :], 1.5, y32[:, :], ALU.add, ALU.mult)
                    ins.then_inc(rstd_ready if k == 13 else rstd_step, 1)

            per_tok = lambda ap: ap.unsqueeze(2).broadcast_to([P, TOK, E])
            per_expert = lambda ap: ap.unsqueeze(1).broadcast_to([P, TOK, E])

            def pick(s, k1, k3, ks):
                r2 = per_tok(rr[:, k3 % 2, 0:TOK])
                tt, ttr = dve.tensor_tensor, dve.tensor_reduce
                for k in ks:
                    if k == 1:
                        dve.wait_ge(rstd_ready, s + 4)
                    else:
                        dve.wait_ge(pick_step, (s + 1) * PICK_OPS + k - 1)
                    if k == 1:
                        ins = tt(lo[:, :, :], lg[:, k1 % 2, :, :], r2, ALU.mult)
                    elif k == 2:
                        ins = tt(lo[:, :, :], lo[:, :, :], per_expert(router_bias[:, :]), ALU.add)
                    elif k == 3:
                        ins = ttr(m1[:, :], lo[:, :, :], AX.X, ALU.max)
                    elif k == 4:
                        ins = tt(o1[:, :, :], lo[:, :, :], per_tok(m1[:, :]), ALU.is_equal)
                    elif k == 5:
                        ins = tt(o1[:, :, :], o1[:, :, :], per_expert(order[:, :]), ALU.mult)
                    elif k == 6:
                        ins = ttr(pm[:, :], o1[:, :, :], AX.X, ALU.max)
                    elif k == 7:
                        ins = tt(o1[:, :, :], o1[:, :, :], per_tok(pm[:, :]), ALU.is_equal)
                    elif k == 8:
                        ins = dve.scalar_tensor_tensor(l2[:, :, :], o1[:, :, :], -BIG, lo[:, :, :], ALU.mult, ALU.add)
                    elif k == 9:
                        ins = ttr(m2[:, :], l2[:, :, :], AX.X, ALU.max)
                    elif k == 10:
                        ins = tt(lo[:, :, :], l2[:, :, :], per_tok(m2[:, :]), ALU.is_equal)
                    elif k == 11:
                        ins = tt(lo[:, :, :], lo[:, :, :], per_expert(order[:, :]), ALU.mult)
                    elif k == 12:
                        ins = ttr(pm[:, :], lo[:, :, :], AX.X, ALU.max)
                    elif k == 13:
                        ins = tt(lo[:, :, :], lo[:, :, :], per_tok(pm[:, :]), ALU.is_equal)
                    elif k == 14:
                        ins = tt(dd[:, :], m1[:, :], m2[:, :], ALU.subtract)
                    elif k == 15:
                        dve.wait_ge(soft_ready, s + 2)
                        ins = tt(o1[:, :, :], o1[:, :, :], per_tok(ws[:, 0, :]), ALU.mult)
                    elif k == 16:
                        ins = tt(lo[:, :, :], lo[:, :, :], per_tok(ws[:, 1, :]), ALU.mult)
                    elif k == 17:
                        ins = tt(o1[:, :, :], o1[:, :, :], lo[:, :, :], ALU.add)
                    elif k == 18:
                        ins = tt(l2[:, :, :], o1[:, :, :], r2, ALU.mult)
                    elif k == 19:
                        if after(s, 0):
                            dve.wait_ge(pack_turned, s * 2 + 2)
                        ins = dve.tensor_copy(pk[:, :, 0:E], l2[:, :, :])
                    elif k == 20:
                        ins = tt(pk[:, :, E:2 * E], l2[:, :, :], pk[:, :, 0:E].bitcast(F32), ALU.subtract)
                    elif k == 21:
                        ins = dve.tensor_copy(pk[:, :, 2 * E:3 * E], o1[:, :, :])
                    else:
                        ins = tt(pk[:, :, 3 * E:4 * E], o1[:, :, :], pk[:, :, 2 * E:3 * E].bitcast(F32), ALU.subtract)
                    ins.then_inc(pick_step, 1)

            def scale(e, u, k, h):
                dve.wait_ge(bcast_ready, u * E + e + 1)
                if after(u, 1) or e >= NZ:
                    dve.wait_ge(expert_done, u * E + e - NZ + 1)
                dve.tensor_tensor(zb[:, e % NZ, :], ring[:, bcast_bank(h, e), :], x2t[:, k % 3, h, :], ALU.mult).then_inc(z_dve, 1)

            def total(u, k, h):
                dve.wait_ge(expert_done, u * E + E)
                dve.tensor_tensor(x2t[:, k % 3, h, :], b_m[:, :], x2t[:, k % 3, h, :], ALU.add).then_inc(sum_done, 1)

            def gated(v):
                dve.wait_ge(gate_ready, v + 1)
                dve.tensor_tensor(sig_c[:, :], b_t[:, :], sig_c[:, :], ALU.mult).then_inc(om_done, 1)

            def residual(v, k, h):
                dve.wait_ge(om_done, v + 1)
                if after(v, 6):
                    dve.wait_ge(y_turned, v - 5)
                dve.tensor_tensor(x2t[:, k % 3, h, :], b_x[:, :], sig_c[:, :], ALU.add).then_inc(x2_ready, 1)

            def back(v, k, h):
                dve.wait_ge(back_ready, v + 1)
                for j in range(JP):
                    dve.bn_stats(bst_x[:, k % 2, h * JP + j, :], b_d[:, j * P:j * P + P].rearrange("p (t c) -> p c t", t=2))
                dve.tensor_copy(lg[:, k % 2, h * UNIT_J:(h + 1) * UNIT_J, :].rearrange("p j e -> p (j e)"),
                                b_l[:, 0:UNIT_J * E]).then_inc(back_done, 1)

            def step_c(s, k, ahead=True, route=True, experts=True, stats=True):
                for h in range(2):
                    u = s * 2 + h
                    v = u + 4
                    if experts:
                        scale(0, u, k, h)
                        if after(u, 1):
                            total(u - 1, k if h else k - 1, 1 - h)
                        scale(1, u, k, h)
                    if route:
                        rstd_c(s, k + 3, range(0, 5)) if h == 0 else pick(s, k + 1, k + 3, range(4, 8))
                    if experts:
                        scale(2, u, k, h)
                    if ahead:
                        gated(v)
                    if route:
                        rstd_c(s, k + 3, range(5, 8)) if h == 0 else pick(s, k + 1, k + 3, range(8, 11))
                    if ahead:
                        residual(v, k + 2, h)
                    if route:
                        rstd_c(s, k + 3, range(8, 11)) if h == 0 else pick(s, k + 1, k + 3, range(11, 15))
                    if experts:
                        scale(4, u, k, h)
                    if stats and h == 1:
                        stats_t(s + 4, range(0, 4))
                    if route:
                        rstd_c(s, k + 3, range(11, 14)) if h == 0 else pick(s, k + 1, k + 3, range(15, 19))
                    if ahead:
                        back(v, k + 2, h)
                    if experts:
                        scale(5, u, k, h)
                    if stats and h == 1:
                        stats_t(s + 4, range(4, 8))
                    if route:
                        pick(s, k + 1, k + 3, range(1, 4) if h == 0 else range(19, 23))
                    if experts:
                        scale(7, u, k, h)

            stats_t(0, range(8))
            rstd_c(-3, 0, range(RSTD_OPS))
            stats_t(1, range(8))
            rstd_c(-2, 1, range(RSTD_OPS))
            step_c(-2, -2, route=False, experts=False)
            step_c(-1, -1, experts=False)
            for s in range(HEAD):
                step_c(s, s)
            with dve.Fori(0, LOOPS) as i:
                for k in range(HEAD, HEAD + CYCLE):
                    step_c(i * CYCLE + k, k)
            for s in range(TAIL, STEPS):
                step_c(s, s, ahead=s + 2 < STEPS, route=s + 1 < STEPS, stats=s + 4 < STEPS)
            total(2 * STEPS - 1, STEPS - 1, 1)


_CONV = ["ln_in_w", "ln_in_b", "ln_c_w", "ln_c_b"] + [p + s for p in PROJ for s in ("_w", "_b")]


def kernel(**inputs):
    import numpy as _np
    import concourse.bacc as _bacc
    from concourse.bass_utils import run_bass_kernel_spmd as _run

    nc = _bacc.Bacc("TRN2", target_bir_lowering=False, num_devices=1)
    arrays, aps = {}, {}
    for name, value in inputs.items():
        a = _np.ascontiguousarray(value)
        arrays[f"in_{name}"] = a
        aps[name] = nc.dram_tensor(f"in_{name}", a.shape, mybir.dt.from_np(a.dtype), kind="ExternalInput").ap()
    out = nc.dram_tensor("out_0", (1, N, N, C), F32, kind="ExternalOutput").ap()
    metaformer_kernel(nc, aps["x"], aps["L0_conv_mask"], {n: aps["L0_conv_" + n] for n in _CONV},
                      aps["L0_ffn_router_w"], aps["L0_ffn_router_b"], aps["L0_ffn_expert_w"], aps["L0_ffn_expert_b"], out)
    return _run(nc, [arrays], core_ids=[0]).results[0]["out_0"]
```

```python
from contextlib import ExitStack

import concourse.bass as bass
from concourse import mybir

F32 = mybir.dt.float32
F32R = mybir.dt.float32r
I32 = mybir.dt.int32
ALU = mybir.AluOpType
ACT = mybir.ActivationFunctionType
AX = mybir.AxisListType

P = 128
N = 256
C = 64
E = 8
Q = 2
ROWS = 16
BLOCKS = N // ROWS
GROUP = 4
GROUPS = ROWS // GROUP
CHUNK = 8
CHUNKS = C // CHUNK
RUN = CHUNK * ROWS
UNIT_J = 8
STEP_J = 2 * UNIT_J
STEPS = 2 * N // STEP_J
JP = UNIT_J // 2
WIDE = JP * P
CYCLE = 6
HEAD = 4
LOOPS = (STEPS - 2 * HEAD) // CYCLE
TAIL = HEAD + LOOPS * CYCLE
TOK = STEP_J
ROUTE = 4 * E
EP = E // 2
TILES = 2 * EP
POOL_TILES = (1, 3, 5)
DVE_TILES = tuple(m for m in range(TILES) if m not in POOL_TILES)
ND, NP_ = len(DVE_TILES), len(POOL_TILES)
NZ = 4
UNITS = 2 * STEPS
X2 = 6
XC = 3
EPS_LN = 1e-5
EPS_OUTER = 1e-6
SEED = float(0x5F3759DF)
BIG = 3e38
PROJ = ["left_proj", "right_proj", "left_gate", "right_gate", "gating", "out_proj"]
LRG = 4 * C
RSTD_OPS = 14
PICK_OPS = 19
STAT_OPS_A = 13
BACK = P + 2 * E
RING_USES = [[("bcast", m) for m in range(2, TILES)] + [("y", 0)] + pack + [("bcast", 0), ("bcast", 1)]
             for pack in ([], [("pack", 0), ("pack", 1)])]


def ring_bank(h, kind, m):
    return (h * len(RING_USES[0]) + RING_USES[h].index((kind, m))) % 2


def bcast_bank(h, m):
    return ring_bank(1 - h if m < 2 else h, "bcast", m)


def y_bank(h):
    return ring_bank(1 - h, "y", 0)


def pack_bank(w):
    return ring_bank(1, "pack", w)


def after(n, k):
    return not isinstance(n, int) or n >= k


def has(u):
    return not isinstance(u, int) or 0 <= u < UNITS


def metaformer_kernel(nc, x, mask, weights, router_w, router_b, expert_w, expert_b, out):
    lr_dram = nc.dram_tensor("left_right_scratch", [BLOCKS, P, Q * 2 * C * ROWS], F32, kind="Internal").ap()
    x_rows = x.rearrange("a (b r) (p q) c -> (a b) p r (q c)", r=ROWS, q=Q)
    x_units = x.rearrange("a (h p) (u j) c -> (a h) u p j c", p=P, j=UNIT_J)
    out_units = out.rearrange("a (h p) (u j) c -> (a h) u p j c", p=P, j=UNIT_J)
    HALF = UNITS // 2

    with ExitStack() as ctx:
        def sem(name):
            return ctx.enter_context(nc.semaphore(name))

        def keep(name, shape, dt=F32):
            return ctx.enter_context(nc.sbuf_tensor(name, shape, dt))

        turn_route = keep("turn_route", [P, BACK])
        ident = turn_route[:, 0:P]
        w_router = turn_route[:, P:BACK]
        w_exp = keep("w_exp", [P, EP, C])
        w_og = keep("w_og", [P, 2, P])
        bias_hi = keep("bias_hi", [P, 2, P], F32R)
        bias_lo = keep("bias_lo", [P, 2, P], F32R)
        router_bias = keep("router_bias", [P, E])
        order = keep("order", [P, E])
        rx = keep("rx", [P, 2 * N])
        bx = keep("bx", [P, 2 * N])

        def layer(tensors, psums=()):
            made = []
            with ExitStack() as c:
                for name, shape, *dt in tensors:
                    made.append(c.enter_context(nc.sbuf_tensor(name, shape, *(dt or [F32]))))
                for name, shape in psums:
                    made.append(c.enter_context(nc.psum_tensor(name, shape, F32)))
            return made

        (w_nat, ln_col, bias_row, w_diff, ones, e_nat, r_nat, eb_wide, mask_in) = layer([
            ("w_nat", [C, 6, 2, C]), ("ln_col", [P, 4]), ("bias_row", [1, 6 * C]), ("w_diff", [P, 6 * C]),
            ("ones", [P, P]), ("e_nat", [P, E, C]), ("r_nat", [P, E]), ("eb_wide", [P, 2, P]),
            ("mask_in", [P, 2, N])])
        setup_bytes = 4 * (12 * C + 4 + 6 * C + 6 * C + P + E * C + E + 2 * P + 2 * N)
        (_, w_proj, w_lr, mt, r_all, b_all, xa, xh, xts, sig_a, stage, bst, nv, ny, nt) = layer([
            ("skip_setup", [P, setup_bytes // 4 + 128]),
            ("w_proj", [P, 6 * C]),
            ("w_left_right", [P, Q, LRG]),
            ("mt", [P, N, Q]), ("r_all", [P, N, Q]), ("b_all", [P, N, Q]),
            ("xa", [P, 2, ROWS, Q * C]), ("xh", [P, 2, ROWS, Q * C]), ("xts", [P, 2, GROUP * P]),
            ("sig_a", [P, GROUP, Q, 2 * C]), ("stage", [P, 2, Q, 2 * CHUNKS, ROWS, CHUNK]),
            ("bst", [P, ROWS, 6]), ("nv", [P, ROWS * Q]), ("ny", [P, ROWS * Q]), ("nt", [P, ROWS * Q])])
        (ps_set,) = layer([], [("ps_set", [P, 8, 512])])
        (xt_a, pr_a) = layer([], [("xt_a", [P, 2, 512]), ("pr_a", [P, GROUP, Q * LRG])])

        (t_all, chunk) = layer([("t_all", [P, C, 2 * N]), ("chunk", [P, 2, 2 * Q, BLOCKS, RUN])])
        (ein,) = layer([], [("ein", [P, 4, 512])])

        (_, sel, xc, xn, tn, ttn, xtn, sig_c, x2t, x2d, zb, bcs, wt, outc, bst_t, bst_x, v32, y32, t32, rr, bt, lg, lo, gg,
         oo, m1, m2, pm, dd, ws, pk) = layer([
            ("t_keep", [P, C, 2 * N]),
            ("sel", [P, 2, 2, E, C], F32R),
            ("xc", [P, XC, UNIT_J, C]), ("xn", [P, UNIT_J, C]), ("tn", [P, UNIT_J, C]),
            ("ttn", [P, WIDE]), ("xtn", [P, WIDE]), ("sig_c", [P, WIDE]), ("x2t", [P, X2, WIDE]), ("x2d", [P, 2, 2, WIDE]),
            ("zb", [P, NZ, WIDE]), ("bcs", [P, 2, WIDE]), ("wt", [P, 2, 2, WIDE // 2], F32R),
            ("outc", [P, 2, UNIT_J, C]), ("bst_t", [P, TOK // 2, 6]), ("bst_x", [P, 2, TOK // 2, 6]),
            ("v32", [P, 2 * TOK]), ("y32", [P, 2 * TOK]), ("t32", [P, 2 * TOK]), ("rr", [P, 2, 2 * TOK]),
            ("bt", [P, 2, TOK]), ("lg", [P, 2, TOK, E]), ("lo", [P, TOK, E]), ("gg", [P, TOK, 2, E]),
            ("oo", [P, 2, TOK, E]), ("m1", [P, TOK]), ("m2", [P, TOK]), ("pm", [P, TOK]),
            ("dd", [P, TOK]), ("ws", [P, 2, TOK]), ("pk", [P, TOK, 2, 2, E], F32R)])
        (b_t, b_g, b_x, b_d, b_m, ring) = layer([], [
            ("b_t", [P, 512]), ("b_g", [P, 512]), ("b_x", [P, 512]), ("b_d", [P, 2, 512]),
            ("b_m", [P, 512]), ("ring", [P, 2, 512])])

        set_step = sem("set_step"); w_in = sem("w_in"); id_made = sem("id_made"); pool_const = sem("pool_const")
        set_pe = sem("set_pe"); set_dve = sem("set_dve"); set_act = sem("set_act")
        x_in = [sem("x_in0"), sem("x_in1")]
        stats_ready = sem("stats_ready"); stat_step = sem("stat_step")
        xh_step = sem("xh_step"); xh_ready = sem("xh_ready")
        xt_ready = sem("xt_ready"); xts_ready = sem("xts_ready"); proj_ready = sem("proj_ready")
        sig_ready = sem("sig_ready"); lr_done = sem("lr_done"); stored = [sem("stored0"), sem("stored1")]
        turn_ready = sem("turn_ready"); turned = sem("turned")
        chunk_in = [sem("chunk_in0"), sem("chunk_in1")]
        ein_ready = sem("ein_ready"); ein_act = sem("ein_act"); ein_dve = sem("ein_dve")
        xc_in = [sem("xc_in0"), sem("xc_in1"), sem("xc_in2")]; sel_made = sem("sel_made")
        rstd_step = sem("rstd_step"); rstd_ready = sem("rstd_ready"); bn_t_done = sem("bn_t_done")
        norm_step = sem("norm_step"); norm_ready = sem("norm_ready")
        turns_ready = sem("turns_ready"); turns_out = sem("turns_out"); g_ready = sem("g_ready"); og_ready = sem("og_ready"); dup_ready = sem("dup_ready")
        gate_ready = sem("gate_ready"); om_done = sem("om_done"); x2_ready = sem("x2_ready")
        back_ready = sem("back_ready"); back_done = sem("back_done")
        pick_step = sem("pick_step"); soft_ready = sem("soft_ready")
        pack_turned = sem("pack_turned"); pack_out = sem("pack_out")
        bcast_ready = sem("bcast_ready"); bcast_out = sem("bcast_out")
        z_dve = sem("z_dve"); z_pool = sem("z_pool"); expert_done = sem("expert_done")
        sum_done = sem("sum_done"); y_turned = sem("y_turned"); y_out = sem("y_out")
        out_stored = [sem("out_stored0"), sem("out_stored1")]

        block = ctx.enter_context(nc.Block())
        NW = 40

        @block.sync
        def _(sp):
            for k, name in enumerate(PROJ):
                for half in range(2):
                    sp.dma_start(w_nat[:, k, half, :], weights[name + "_w"]).then_inc(w_in, 16)
                sp.dma_start(bias_row[:, k * C:(k + 1) * C],
                             weights[name + "_b"].rearrange("(a c) -> a c", a=1)).then_inc(w_in, 16)
            for half in range(2):
                part = slice(half * C, half * C + C)
                for col, name in enumerate(["ln_in_w", "ln_c_w"]):
                    sp.dma_start(ln_col[part, 2 * col:2 * col + 1],
                                 weights[name].rearrange("(c a) -> c a", a=1)).then_inc(w_in, 16)
                for col, name in enumerate(["ln_in_b", "ln_c_b"]):
                    sp.dma_start(ln_col[part, 2 * col + 1:2 * col + 2],
                                 weights[name].rearrange("(c a) -> c a", a=1)).then_inc(w_in, 16)
                sp.dma_start(e_nat[part, :, :], expert_w.rearrange("e d c -> d e c")).then_inc(w_in, 16)
                sp.dma_start(r_nat[part, :], router_w).then_inc(w_in, 16)
            sp.dma_start(router_bias[:, :], router_b.rearrange("(a e) -> a e", a=1).broadcast_to([P, E])).then_inc(w_in, 16)
            sp.dma_start(mask_in[:, :, :], mask.rearrange("a (h p) k -> p (a h) k", p=P)).then_inc(w_in, 16)
            sp.wait_ge(pool_const, 3)
            for t in range(4):
                for part in range(2):
                    row = t * ROUTE + (2 + part) * E
                    half = t % 2
                    sp.dma_start(eb_wide[row:row + E, t // 2, half * C:half * C + C], expert_b).then_inc(w_in, 16)

            def load_x(n, b):
                if after(n, 2):
                    sp.wait_ge(xh_ready, n - 1)
                sp.dma_start(xa[:, b, :, :], x_rows[n]).then_inc(x_in[b], 16)

            def block_a(n, b, last=False):
                if not last:
                    load_x(n + 3, 1 - b)
                sp.wait_ge(lr_done, (n + 1) * ROWS)
                sp.dma_start(lr_dram[n], stage[:, b, :, :, :, :].rearrange("p q s r c -> p (q s r c)")).then_inc(stored[b], 16)

            load_x(0, 0)
            load_x(1, 1)
            load_x(2, 0)
            for n in range(BLOCKS):
                block_a(n, n % 2, n + 3 >= BLOCKS)

            for b in range(2):
                sp.wait_ge(stored[b], 16 * BLOCKS // 2)
            sp.wait_ge(turned, 1)

            def load_chunk(c, b):
                if after(c, 2):
                    sp.wait_ge(ein_ready, (c - 1) * CHUNK)
                for u in range(2 * Q):
                    part = lr_dram.rearrange("n p (u c) -> u p n c", u=2 * Q)[u, :, :, c * RUN:(c + 1) * RUN]
                    sp.dma_start(chunk[:, b, u, :, :], part).then_inc(chunk_in[b], 16)

            for c in range(CHUNKS):
                load_chunk(c, c % 2)
            sp.wait_ge(ein_ready, C)

            def load_unit(v, kv):
                if after(v, XC):
                    sp.wait_ge(turns_ready, v - XC + 1)
                sp.dma_start(xc[:, kv % XC, :, :], x_units[v // HALF, v % HALF]).then_inc(xc_in[kv % XC], 16)

            def store_unit(u, ku):
                sp.wait_ge(y_out, u + 1)
                sp.dma_start(out_units[u // HALF, u % HALF], outc[:, ku % 2, :, :]).then_inc(out_stored[ku % 2], 16)

            def slot(u, ku):
                if has(u + 6):
                    load_unit(u + 6, ku + 6)
                if has(u - 1):
                    store_unit(u - 1, ku - 1)

            for v in range(XC):
                load_unit(v, v)
            for u in range(XC - 6, 2 * HEAD):
                slot(u, u)
            with sp.Fori(0, LOOPS) as i:
                for k in range(2 * HEAD, 2 * (HEAD + CYCLE)):
                    slot(i * (2 * CYCLE) + k, k)
            for u in range(2 * TAIL, UNITS + 1):
                slot(u, u)
            for h in range(2):
                sp.wait_ge(out_stored[h], 16 * UNITS // 2)

        @block.gpsimd
        def _(pool):
            pool.memset(ident[:, :], 0.0).then_inc(id_made, 1)
            pool.memset(ones[:, :], 1.0 / C).then_inc(pool_const, 1)
            pool.memset(w_router, 0.0).then_inc(pool_const, 1)
            pool.memset(eb_wide[:, :, :], 0.0).then_inc(pool_const, 1)
            pool.memset(w_og[:, :, :], 0.0).then_inc(pool_const, 1)
            pool.memset(w_lr[:, :, :], 0.0).then_inc(pool_const, 1)
            for e in range(E):
                m = pool.memset(order[:, e:e + 1], float(E - e))
            m.then_inc(pool_const, 1)
            pool.wait_ge(id_made, 1)
            pool.affine_select(out=ident[:, :], in_=ident[:, :], compare_op=ALU.not_equal, fill=1.0, base=0,
                               pattern=[[-1, P]], channel_multiplier=1).then_inc(id_made, 1)

            def block_a(n, b):
                rows = bass.ts(n, ROWS)
                src = xa[:, b, :, :].rearrange("p r (q c) -> p (r q) c", q=Q)
                dst = xh[:, b, :, :].rearrange("p r (q c) -> p (r q) c", q=Q)
                r = r_all[:, rows, :].rearrange("p r q -> p (r q)").unsqueeze(2).broadcast_to([P, ROWS * Q, C])
                m = b_all[:, rows, :].rearrange("p r q -> p (r q)").unsqueeze(2).broadcast_to([P, ROWS * Q, C])
                pool.wait_ge(stats_ready, n + 1)
                if after(n, 2):
                    pool.wait_ge(xt_ready, (n - 1) * GROUPS)
                pool.tensor_tensor(dst, src, r, ALU.mult).then_inc(xh_step, 1)
                pool.wait_ge(xh_step, n + 1)
                pool.tensor_tensor(dst, dst, m, ALU.add).then_inc(xh_ready, 1)

            block_a(0, 0)
            block_a(1, 1)
            with pool.Fori(1, BLOCKS // 2) as i:
                block_a(i * 2, 0)
                block_a(i * 2 + 1, 1)

            def norm(v, kv, between=lambda: None):
                pool.wait_ge(xc_in[kv % XC], (v - kv % XC) // XC * 16 + 16)
                h, b = kv % 2, kv // 2 % 2
                s = (v - h) // 2
                pool.wait_ge(rstd_ready, s + 1)
                if after(v, 1):
                    pool.wait_ge(turns_ready, v)
                cols = slice(h * UNIT_J, h * UNIT_J + UNIT_J)
                t_in = t_all[:, :, bass.ts(v, UNIT_J)].rearrange("p c j -> p j c")
                r_t = rr[:, b, TOK + h * UNIT_J:TOK + (h + 1) * UNIT_J].unsqueeze(2).broadcast_to([P, UNIT_J, C])
                b_tt = bt[:, b, cols].unsqueeze(2).broadcast_to([P, UNIT_J, C])
                r_x = rx[:, bass.ts(v, UNIT_J)].unsqueeze(2).broadcast_to([P, UNIT_J, C])
                b_xx = bx[:, bass.ts(v, UNIT_J)].unsqueeze(2).broadcast_to([P, UNIT_J, C])
                pool.tensor_tensor(xn[:, :, :], xc[:, kv % XC, :, :], r_x, ALU.mult).then_inc(norm_step, 1)
                pool.tensor_tensor(tn[:, :, :], t_in, r_t, ALU.mult).then_inc(norm_step, 1)
                between()
                pool.wait_ge(norm_step, v * 2 + 1)
                pool.tensor_tensor(xn[:, :, :], xn[:, :, :], b_xx, ALU.add)
                pool.wait_ge(norm_step, v * 2 + 2)
                pool.tensor_tensor(tn[:, :, :], tn[:, :, :], b_tt, ALU.add).then_inc(norm_ready, 1)

            def scale(m, u, ku):
                i = POOL_TILES.index(m)
                pool.wait_ge(bcast_out, u * NP_ + i + 1)
                if i == 0:
                    pool.wait_ge(dup_ready, u + 1)
                if after(u, 1) or m >= NZ:
                    pool.wait_ge(expert_done, u * EP + m // 2 - 1)
                pool.tensor_tensor(zb[:, m % NZ, :], bcs[:, (ku * NP_ + i) % 2, :], x2d[:, ku % 2, m % 2, :], ALU.mult)\
                    .then_inc(z_pool, 1)

            def slot(u, ku):
                if has(u):
                    scale(3, u, ku)
                if has(u + 5):
                    norm(u + 5, ku + 5, lambda: scale(5, u, ku) if has(u) else None)
                elif has(u):
                    scale(5, u, ku)
                if has(u + 1):
                    scale(1, u + 1, ku + 1)

            pool.wait_ge(ein_ready, (CHUNKS - 1) * CHUNK)
            kinds = ident[:, :].rearrange("p (t k e) -> p t k e", t=4, k=4)
            for t in range(4):
                ins = pool.tensor_tensor(sel[:, t // 2, t % 2, :, :],
                                         kinds[:, t, 0, :].unsqueeze(2).broadcast_to([P, E, C]),
                                         kinds[:, t, 1, :].unsqueeze(2).broadcast_to([P, E, C]), ALU.add)
            ins.then_inc(sel_made, 1)
            pool.wait_ge(ein_ready, C)
            norm(0, 0)
            for u in range(-4, 2 * HEAD):
                slot(u, u)
            with pool.Fori(0, LOOPS) as i:
                for k in range(2 * HEAD, 2 * (HEAD + CYCLE)):
                    slot(i * (2 * CYCLE) + k, k)
            for u in range(2 * TAIL, UNITS):
                slot(u, u)

        @block.scalar
        def _(act):
            act.wait_ge(set_pe, 2)
            for h in range(2):
                for q in range(Q):
                    ins = act.activation(mt[:, h * P:h * P + P, q], ps_set[:, 1, (2 * h + q) * P:(2 * h + q + 1) * P], ACT.Copy)
            ins.then_inc(set_act, 1)

            def evacuate(n, g, b):
                act.wait_ge(xt_ready, n * GROUPS + g + 1)
                if after(n, 1) or g >= 2:
                    act.wait_ge(proj_ready, (n * GROUPS + g - 1) * GROUP)
                act.activation(xts[:, g % 2, :], xt_a[:, g % 2, :], ACT.Copy).then_inc(xts_ready, 1)

            def gates(n, g):
                for r in range(GROUP):
                    act.wait_ge(proj_ready, (n * GROUPS + g) * GROUP + r + 1)
                    act.activation(sig_a[:, r, :, :], pr_a[:, r, :].rearrange("p (q c) -> p q c", q=Q)[:, :, 2 * C:4 * C],
                                   ACT.Sigmoid).then_inc(sig_ready, 1)

            def block_a(n, b, last=False):
                for g in range(GROUPS):
                    if g < GROUPS - 1:
                        evacuate(n, g + 1, b)
                    elif not last:
                        evacuate(n + 1, 0, b)
                    gates(n, g)

            evacuate(0, 0, 0)
            block_a(0, 0)
            block_a(1, 1)
            with act.Fori(1, BLOCKS // 2 - 1) as i:
                block_a(i * 2, 0)
                block_a(i * 2 + 1, 1)
            block_a(BLOCKS - 2, 0)
            block_a(BLOCKS - 1, 1, True)
            act.wait_ge(turn_ready, 1)
            for k, dst in enumerate([rx, bx]):
                for h in range(2):
                    for q in range(Q):
                        ins = act.activation(dst[:, h * N:h * N + N].rearrange("p (j q) -> p j q", q=Q)[:, :, q],
                                             pr_a[:, k, (2 * h + q) * P:(2 * h + q + 1) * P], ACT.Copy)
            ins.then_inc(turned, 1)

            def chunk_b(c):
                for k in range(0, CHUNK, 2):
                    act.wait_ge(ein_ready, c * CHUNK + k + 1)
                    act.activation(t_all[:, bass.ds(c * CHUNK + k, 1), :].rearrange("p a n -> p (a n)"),
                                   ein[:, k % 4, :], ACT.Copy).then_inc(ein_act, 1)

            with act.Fori(0, CHUNKS) as c:
                chunk_b(c)

            def front(v):
                act.wait_ge(turns_ready, v + 1)
                if after(v, 1):
                    act.wait_ge(og_ready, v)
                act.activation(xtn[:, :], b_g[:, :], ACT.Copy)
                act.activation(ttn[:, :], b_t[:, :], ACT.Copy).then_inc(turns_out, 1)

            def gate(v):
                act.wait_ge(g_ready, v + 1)
                if after(v, 1):
                    act.wait_ge(x2_ready, v)
                act.activation(sig_c[:, :], b_g[:, :], ACT.Sigmoid).then_inc(gate_ready, 1)

            def double(w, kw, t):
                if t == 0:
                    act.wait_ge(x2_ready, w + 1)
                    if after(w, 2):
                        act.wait_ge(z_dve, (w - 1) * ND)
                        act.wait_ge(z_pool, (w - 1) * NP_)
                for half in range(2):
                    ins = act.activation(x2d[half * C:(half + 1) * C, kw % 2, t, :], x2t[t * C:(t + 1) * C, kw % X2, :], ACT.Copy)
                if t == 1:
                    ins.then_inc(dup_ready, 1)

            def y_evacuate(u, ku):
                act.wait_ge(y_turned, u + 1)
                h = ku % 2
                if after(u, 2):
                    act.wait_ge(out_stored[h], (u - h) * 8)
                act.activation(outc[:, h, :, :].rearrange("p j c -> p (j c)"), ring[:, y_bank(h), :], ACT.Copy)\
                   .then_inc(y_out, 1)

            def bcast(m, u, ku):
                i = POOL_TILES.index(m)
                act.wait_ge(bcast_ready, u * TILES + m + 1)
                if after(u, 1) or i >= 2:
                    act.wait_ge(z_pool, u * NP_ + i - 1)
                act.activation(bcs[:, (ku * NP_ + i) % 2, :], ring[:, bcast_bank(ku % 2, m), :], ACT.Copy).then_inc(bcast_out, 1)

            def soft(s):
                act.wait_ge(pick_step, (s + 1) * PICK_OPS + 10)
                act.activation(ws[:, 0, :], dd[:, :], ACT.Sigmoid)
                act.activation(ws[:, 1, :], dd[:, :], ACT.Sigmoid, scale=-1.0).then_inc(soft_ready, 1)

            def pack(w, kw):
                act.wait_ge(pack_turned, w + 1)
                act.activation(wt[:, kw // 2 % 2, kw % 2, :], ring[:, pack_bank(kw % 2), 0:WIDE // 2], ACT.Copy).then_inc(pack_out, 1)

            def slot(u, ku):
                odd = ku % 2 == 1
                if has(u):
                    bcast(3, u, ku)
                if odd and has(u + 1):
                    soft((u - 1) // 2)
                if has(u + 4):
                    front(u + 4)
                if has(u + 1):
                    double(u + 1, ku + 1, 0)
                if has(u):
                    bcast(5, u, ku)
                if has(u + 1):
                    double(u + 1, ku + 1, 1)
                if has(u + 4):
                    gate(u + 4)
                if has(u - 1):
                    y_evacuate(u - 1, ku - 1)
                if odd and has(u + 1):
                    pack(u + 1, ku + 1)
                    pack(u + 2, ku + 2)
                if has(u + 1):
                    bcast(1, u + 1, ku + 1)

            for u in range(-4, 2 * HEAD):
                slot(u, u)
            with act.Fori(0, LOOPS) as i:
                for k in range(2 * HEAD, 2 * (HEAD + CYCLE)):
                    slot(i * (2 * CYCLE) + k, k)
            for u in range(2 * TAIL, UNITS + 1):
                slot(u, u)

        @block.tensor
        def _(pe):
            pe.wait_ge(id_made, 2)
            pe.wait_ge(w_in, 16 * NW)
            for k in range(6):
                m = pe.transpose(ps_set[:, 0, k * C:(k + 1) * C], w_nat[:, k, :, :].rearrange("p a c -> p (a c)"), ident[0:C, 0:C])
            m.then_inc(set_pe, 1)
            for h in range(2):
                for q in range(Q):
                    m = pe.transpose(ps_set[:, 1, (2 * h + q) * P:(2 * h + q + 1) * P],
                                     mask_in[:, h, :].rearrange("p (k q) -> p k q", q=Q)[:, :, q], ident[:, :])
            m.then_inc(set_pe, 1)
            pe.matmul(ps_set[:, 2, :], ones[0:C, :], e_nat[0:C, :, :].rearrange("p e c -> p (e c)"), start=True, stop=True)
            pe.matmul(ps_set[:, 3, 0:E], ones[0:C, :], r_nat[0:C, :], start=True, stop=True).then_inc(set_pe, 1)
            pe.wait_ge(set_dve, 1)
            pe.matmul(ps_set[:, 4, 0:6 * C], ones[0:C, :], w_diff[0:C, :], start=True, stop=False)
            pe.matmul(ps_set[:, 4, 0:6 * C], ones[0:1, :], bias_row[:, :], start=False, stop=True).then_inc(set_pe, 1)
            pe.wait_ge(set_dve, 3)
            pe.wait_ge(set_act, 1)

            def turn(n, g, b):
                pe.wait_ge(xh_ready, n + 1)
                if after(n, 1) or g >= 2:
                    pe.wait_ge(xts_ready, n * GROUPS + g - 1)
                for r in range(GROUP):
                    m = pe.transpose(xt_a[:, g % 2, r * P:(r + 1) * P], xh[:, b, g * GROUP + r, :], ident[:, :])
                m.then_inc(xt_ready, 1)

            def project(n, g):
                pe.wait_ge(xts_ready, n * GROUPS + g + 1)
                for r in range(GROUP):
                    if after(n, 1) or g >= 1:
                        pe.wait_ge(lr_done, (n * GROUPS + g - 1) * GROUP + r + 1)
                    pe.matmul(pr_a[:, r, :], xts[:, g % 2, r * P:(r + 1) * P], w_lr[:, :, :].rearrange("p q c -> p (q c)"),
                              start=True, stop=True).then_inc(proj_ready, 1)

            def block_a(n, b, last=False):
                for g in range(GROUPS):
                    if g < GROUPS - 1:
                        turn(n, g + 1, b)
                    elif not last:
                        turn(n + 1, 0, 1 - b)
                    project(n, g)

            turn(0, 0, 0)
            block_a(0, 0)
            block_a(1, 1)
            with pe.Fori(1, BLOCKS // 2 - 1) as i:
                block_a(i * 2, 0)
                block_a(i * 2 + 1, 1)
            block_a(BLOCKS - 2, 0)
            block_a(BLOCKS - 1, 1, True)
            pe.wait_ge(lr_done, BLOCKS * ROWS)
            for k, src in enumerate([r_all, b_all]):
                for h in range(2):
                    for q in range(Q):
                        m = pe.transpose(pr_a[:, k, (2 * h + q) * P:(2 * h + q + 1) * P],
                                         src[:, h * P:h * P + P, q], ident[:, :])
            m.then_inc(turn_ready, 1)
            pe.wait_ge(turned, 1)

            def chunk_b(c, b):
                pe.wait_ge(chunk_in[b], (c // 2 + 1) * 64 if isinstance(c, int) else (c - b) * 32 + 64)
                for k in range(CHUNK):
                    if after(c, 1) or k >= 4:
                        pe.wait_ge(ein_dve if k % 2 else ein_act, c * (CHUNK // 2) + k // 2 - 1)
                    side = chunk[:, b, :, :, :].rearrange("p u n (r c) -> p u (n r) c", c=CHUNK)[:, :, :, k]
                    for h in range(2):
                        for q in range(Q):
                            m = pe.matmul(ein[:, k % 4, h * N:h * N + N],
                                          side[:, 2 * q, h * P:h * P + P], side[:, 2 * q + 1, :], start=q == 0, stop=q == 1)
                    m.then_inc(ein_ready, 1)

            chunk_b(0, 0)
            chunk_b(1, 1)
            with pe.Fori(1, CHUNKS // 2) as i:
                chunk_b(i * 2, 0)
                chunk_b(i * 2 + 1, 1)
            pe.wait_ge(ein_act, C // 2)
            pe.wait_ge(ein_dve, C // 2)

            pe.wait_ge(sel_made, 1)

            pairs = [slice(j * P, j * P + P) for j in range(JP)]
            of_pair = lambda bank, a: bank.rearrange("p (q a i) -> p q a i", q=2, a=2)[:, :, a, :]

            def turns(v, kv):
                pe.wait_ge(norm_ready, v + 1)
                if after(v, 1):
                    pe.wait_ge(x2_ready, v)
                for dst, src in ((b_g, xn[:, :, :]), (b_t, tn[:, :, :]), (b_x, xc[:, kv % XC, :, :])):
                    for j in range(JP):
                        m = pe.transpose(dst[:, pairs[j]], src[:, 2 * j:2 * j + 2, :].rearrange("p j c -> p (j c)"), ident)
                m.then_inc(turns_ready, 1)

            def out_gate(v):
                pe.wait_ge(turns_out, v + 1)
                pe.matmul(b_g[:, :], w_og[:, 0, :], xtn[:, :], start=True, stop=True).then_inc(g_ready, 1)
                pe.matmul(b_t[:, :], w_og[:, 1, :], ttn[:, :], start=True, stop=True).then_inc(og_ready, 1)

            def back(w, kw):
                pe.wait_ge(x2_ready, w + 1)
                if after(w, 1):
                    pe.wait_ge(back_done, w)
                for j in range(JP):
                    m = pe.matmul(b_d[:, j // 2, j % 2 * BACK:(j % 2 + 1) * BACK], x2t[:, kw % X2, pairs[j]], turn_route[:, :],
                                  start=True, stop=True)
                m.then_inc(back_ready, 1)

            def ring_free(kind, m, u, h):
                r = RING_USES[h].index((kind, m))
                while True:
                    r -= 2
                    if r < 0:
                        u, h = u - 1, 1 - h
                        r += len(RING_USES[h])
                        if isinstance(u, int) and u < -1:
                            return
                    kind, m = RING_USES[h][r]
                    unit = {"bcast": u + 1 if m < 2 else u, "y": u - 1, "pack": u + 1 + m}[kind]
                    if has(unit):
                        break
                if kind == "bcast" and m in DVE_TILES:
                    pe.wait_ge(z_dve, unit * ND + DVE_TILES.index(m) + 1)
                elif kind == "bcast":
                    pe.wait_ge(bcast_out, unit * NP_ + POOL_TILES.index(m) + 1)
                elif kind == "y":
                    pe.wait_ge(y_out, unit + 1)
                else:
                    pe.wait_ge(pack_out, unit + 1)

            def bcast(m, u, ku):
                slot_u, slot_h = (u - 1, 1 - ku % 2) if m < 2 else (u, ku % 2)
                ring_free("bcast", m, slot_u, slot_h)
                if m == 0:
                    pe.wait_ge(pack_out, u + 1)
                for a in range(2):
                    ins = pe.matmul(of_pair(ring[:, bcast_bank(ku % 2, m), :], a),
                                    sel[:, a, m % 2, m // 2 * 2:m // 2 * 2 + 2, :].rearrange("p e c -> p (e c)"),
                                    wt[:, ku // 2 % 2, ku % 2, :], start=True, stop=True)
                ins.then_inc(bcast_ready, 1)

            def bias(u, ku):
                if after(u, 1):
                    pe.wait_ge(sum_done, u)
                for a in range(2):
                    for part, b in enumerate((bias_hi, bias_lo)):
                        pe.matmul(of_pair(b_m[:, :], a), b[:, a, :], wt[:, ku // 2 % 2, ku % 2, :],
                                  start=a == 0 and part == 0, stop=False, skip_group_check=True)

            def expert(ep, u):
                pe.wait_ge(z_dve, u * ND + sum(m <= 2 * ep + 1 for m in DVE_TILES))
                pools = sum(m <= 2 * ep + 1 for m in POOL_TILES)
                if pools:
                    pe.wait_ge(z_pool, u * NP_ + pools)
                for t in range(2):
                    ins = pe.matmul(b_m[t * C:(t + 1) * C, :], w_exp[:, ep, :], zb[:, (2 * ep + t) % NZ, :], start=False,
                                    stop=ep == EP - 1, skip_group_check=True)
                ins.then_inc(expert_done, 1)

            def y_turn(u, ku):
                ring_free("y", 0, u + 1, 1 - ku % 2)
                pe.wait_ge(sum_done, u + 1)
                for j in range(JP):
                    m = pe.transpose(ring[:, y_bank(ku % 2), pairs[j]], x2t[:, ku % X2, pairs[j]], ident)
                m.then_inc(y_turned, 1)

            def pack(s, w):
                ring_free("pack", w, s * 2 + 1, 1)
                pe.wait_ge(pick_step, (s + 1) * PICK_OPS + PICK_OPS)
                for q in range(2):
                    t0 = w * UNIT_J + 4 * q
                    m = pe.transpose(ring[:, pack_bank(w), pairs[q]],
                                     pk[:, t0:t0 + 4, :, :, :].bitcast(F32).rearrange("p j g z e -> p (j g z e)"), ident)
                m.then_inc(pack_turned, 1)

            def slot(u, ku):
                if has(u + 3):
                    back(u + 3, ku + 3)
                if has(u):
                    bcast(2, u, ku)
                    bcast(3, u, ku)
                if has(u + 4):
                    turns(u + 4, ku + 4)
                if has(u):
                    bias(u, ku)
                    expert(0, u)
                    bcast(4, u, ku)
                    bcast(5, u, ku)
                    expert(1, u)
                    bcast(6, u, ku)
                    bcast(7, u, ku)
                if has(u + 4):
                    out_gate(u + 4)
                if has(u - 1):
                    y_turn(u - 1, ku - 1)
                if has(u):
                    expert(2, u)
                if ku % 2 == 1 and has(u + 1):
                    pack((u - 1) // 2, 0)
                    pack((u - 1) // 2, 1)
                if has(u):
                    expert(3, u)
                if has(u + 1):
                    bcast(0, u + 1, ku + 1)
                    bcast(1, u + 1, ku + 1)

            for u in range(-4, 2 * HEAD):
                slot(u, u)
            with pe.Fori(0, LOOPS) as i:
                for k in range(2 * HEAD, 2 * (HEAD + CYCLE)):
                    slot(i * (2 * CYCLE) + k, k)
            for u in range(2 * TAIL, UNITS + 1):
                slot(u, u)

        @block.vector
        def _(dve):
            in5, out1 = slice(0, 5 * C), slice(5 * C, 6 * C)
            dve.wait_ge(set_pe, 1)
            dve.tensor_scalar(w_proj[:, in5], ps_set[:, 0, in5], ln_col[:, 0:1], None, ALU.mult)
            dve.tensor_scalar(w_proj[:, out1], ps_set[:, 0, out1], ln_col[:, 2:3], None, ALU.mult).then_inc(set_step, 1)
            dve.wait_ge(set_step, 1)
            dve.scalar_tensor_tensor(w_diff[:, in5], ps_set[:, 0, in5], ln_col[:, 1:2], w_proj[:, in5], ALU.mult, ALU.subtract)
            dve.scalar_tensor_tensor(w_diff[:, out1], ps_set[:, 0, out1], ln_col[:, 3:4], w_proj[:, out1], ALU.mult, ALU.subtract)\
               .then_inc(set_dve, 1)
            dve.wait_ge(set_pe, 3)
            dve.wait_ge(pool_const, 6)
            for half in range(2):
                part = slice(half * C, half * C + C)
                dve.tensor_tensor(w_exp[part, :, :], e_nat[part, :, :].rearrange("p (e z) c -> p e z c", z=2)[:, :, half, :],
                                  ps_set[part, 2, :].rearrange("p (e z c) -> p e z c", e=EP, z=2)[:, :, half, :], ALU.subtract)
                dve.tensor_tensor(w_router[part, half * E:half * E + E], r_nat[part, :], ps_set[part, 3, 0:E], ALU.subtract)
            dve.tensor_copy(bias_hi[:, :, :], eb_wide[:, :, :]).then_inc(set_step, 1)
            dve.wait_ge(set_step, 2)
            dve.tensor_tensor(bias_lo[:, :, :], eb_wide[:, :, :], bias_hi[:, :, :].bitcast(F32), ALU.subtract)
            dve.wait_ge(set_pe, 4)
            dve.tensor_tensor(w_proj[:, :], w_proj[:, :], ps_set[:, 4, 0:6 * C], ALU.add).then_inc(set_dve, 1)
            dve.wait_ge(set_dve, 2)
            for w in range(2):
                for half in range(2):
                    part = slice(half * C, half * C + C)
                    dve.tensor_copy(w_og[part, w, part], w_proj[part, (4 + w) * C:(5 + w) * C])
            for half in range(2):
                part = slice(half * C, half * C + C)
                ins = dve.tensor_copy(w_lr[part, half, :], w_proj[part, 0:LRG])
            ins.then_inc(set_dve, 1)
            dve.wait_ge(set_act, 1)

            stat_a = bst[:, :, :].rearrange("p r (q z) -> p r q z", q=Q)
            wide = lambda ap: ap[:, :].rearrange("p (r q) -> p r q", q=Q)
            by_chunk = lambda ap: ap.rearrange("p (s c) -> p s c", c=CHUNK)

            def bn(n, b, rows):
                for r in rows:
                    ins = dve.bn_stats(bst[:, r, :], xa[:, b, r, :].rearrange("p (q c) -> p c q", q=Q))
                if rows[-1] == ROWS - 1:
                    ins.then_inc(stat_step, 1)

            def rstd_a(n, ks):
                r_out = r_all[:, bass.ts(n, ROWS), :]
                for k in ks:
                    dve.wait_ge(stat_step, n * STAT_OPS_A + 1 + k)
                    if k == 0:
                        ins = dve.tensor_scalar(wide(nv), stat_a[:, :, :, 2], (1 + EPS_LN) / C, EPS_LN * EPS_OUTER,
                                                ALU.mult, ALU.add)
                    elif k == 1:
                        ins = dve.tensor_scalar(ny[:, :].bitcast(I32), nv[:, :].bitcast(I32), -0.5, SEED, ALU.mult, ALU.add)
                    elif k == 10:
                        ins = dve.scalar_tensor_tensor(r_out, wide(nt), 1.5, wide(ny), ALU.add, ALU.mult)
                    elif k == 11:
                        ins = dve.scalar_tensor_tensor(wide(nt), stat_a[:, :, :, 1], -1.0, r_out, ALU.mult, ALU.mult)
                    elif k == 12:
                        ins = dve.tensor_scalar(b_all[:, bass.ts(n, ROWS), :], wide(nt), 1.0, None, ALU.add)
                    elif k % 3 == 2:
                        ins = dve.tensor_tensor(nt[:, :], ny[:, :], ny[:, :], ALU.mult)
                    elif k % 3 == 0:
                        ins = dve.scalar_tensor_tensor(nt[:, :], nt[:, :], -0.5, nv[:, :], ALU.mult, ALU.mult)
                    else:
                        ins = dve.scalar_tensor_tensor(ny[:, :], nt[:, :], 1.5, ny[:, :], ALU.add, ALU.mult)
                    ins.then_inc(stats_ready if k == 12 else stat_step, 1)

            def wait_x(n, b):
                dve.wait_ge(x_in[b], n // 2 * 16 + 16 if isinstance(n, int) else (n - b) * 8 + 16)

            def left_right(n, row, b):
                dve.wait_ge(sig_ready, n * ROWS + row + 1)
                if row == 0 and after(n, 2):
                    dve.wait_ge(stored[b], n // 2 * 16 if isinstance(n, int) else (n - b) * 8)
                for q in range(Q):
                    ins = dve.scalar_tensor_tensor(
                        stage[:, b, q, :, row, :], by_chunk(pr_a[:, row % GROUP, q * LRG:q * LRG + 2 * C]),
                        mt[:, bass.ds(n * ROWS + row, 1), q], by_chunk(sig_a[:, row % GROUP, q, :]), ALU.mult, ALU.mult)
                ins.then_inc(lr_done, 1)

            def block_a(n, b, ahead=True):
                if ahead:
                    wait_x(n + 2, b)
                for row in range(ROWS):
                    if ahead and row < ROWS // 2:
                        bn(n + 2, b, (2 * row, 2 * row + 1))
                    elif ahead:
                        rstd_a(n + 2, ((0, 1), (2, 3), (4, 5), (6, 7), (8, 9), (10,), (11,), (12,))[row - ROWS // 2])
                    left_right(n, row, b)

            for n in range(2):
                wait_x(n, n)
                bn(n, n, range(ROWS))
                rstd_a(n, range(13))
            block_a(0, 0)
            block_a(1, 1)
            with dve.Fori(1, BLOCKS // 2 - 1) as i:
                block_a(i * 2, 0)
                block_a(i * 2 + 1, 1)
            block_a(BLOCKS - 2, 0, False)
            block_a(BLOCKS - 1, 1, False)

            with dve.Fori(0, CHUNKS) as c:
                for k in range(1, CHUNK, 2):
                    dve.wait_ge(ein_ready, c * CHUNK + k + 1)
                    dve.tensor_copy(t_all[:, bass.ds(c * CHUNK + k, 1), :].rearrange("p a n -> p (a n)"), ein[:, k % 4, :])\
                       .then_inc(ein_dve, 1)
            dve.wait_ge(ein_act, C // 2)
            dve.wait_ge(ein_dve, C // 2)

            def stats_t(s, js):
                for j in js:
                    ins = dve.bn_stats(bst_t[:, j, :], t_all[:, :, bass.ds(s * STEP_J + 2 * j, 2)])
                if js[-1] == TOK // 2 - 1:
                    ins.then_inc(bn_t_done, 1)

            def rstd_c(s, k3, ks):
                b = k3 % 2
                t_stat = bst_t[:, :, :].rearrange("p j (t z) -> p j t z", t=2)
                x_stat = bst_x[:, b, :, :].rearrange("p j (t z) -> p j t z", t=2)
                pair = lambda ap: ap.rearrange("p (j t) -> p j t", t=2)
                for k in ks:
                    if k == 0:
                        if after(s, -1):
                            dve.wait_ge(back_done, s * 2 + 4)
                            dve.wait_ge(norm_ready, s * 2 + 4)
                            ins = dve.tensor_scalar(pair(v32[:, 0:TOK]), x_stat[:, :, :, 2], 1.0 / C, EPS_LN, ALU.mult, ALU.add)
                        else:
                            ins = dve.memset(v32[:, 0:TOK], 1.0)
                    elif k == 1:
                        if not isinstance(s, int) or s + 3 < STEPS:
                            dve.wait_ge(bn_t_done, s + 4)
                        ins = dve.tensor_scalar(pair(v32[:, TOK:2 * TOK]), t_stat[:, :, :, 2], 1.0 / C, EPS_LN, ALU.mult, ALU.add)
                    else:
                        dve.wait_ge(rstd_step, (s + 3) * (RSTD_OPS - 1) + k)
                        if k == 2:
                            ins = dve.tensor_scalar(y32[:, :].bitcast(I32), v32[:, :].bitcast(I32), -0.5, SEED, ALU.mult, ALU.add)
                        elif k == 11:
                            ins = dve.scalar_tensor_tensor(rr[:, b, :], t32[:, :], 1.5, y32[:, :], ALU.add, ALU.mult)
                        elif k == 12:
                            ins = dve.scalar_tensor_tensor(pair(t32[:, 0:TOK]), t_stat[:, :, :, 1], -1.0,
                                                           pair(rr[:, b, TOK:2 * TOK]), ALU.mult, ALU.mult)
                        elif k == 13:
                            ins = dve.tensor_scalar(bt[:, b, :], t32[:, 0:TOK], 1.0, None, ALU.add)
                        elif k % 3 == 0:
                            ins = dve.tensor_tensor(t32[:, :], y32[:, :], y32[:, :], ALU.mult)
                        elif k % 3 == 1:
                            ins = dve.scalar_tensor_tensor(t32[:, :], t32[:, :], -0.5, v32[:, :], ALU.mult, ALU.mult)
                        else:
                            ins = dve.scalar_tensor_tensor(y32[:, :], t32[:, :], 1.5, y32[:, :], ALU.add, ALU.mult)
                    ins.then_inc(rstd_ready if k == 13 else rstd_step, 1)

            per_tok = lambda ap: ap.unsqueeze(2).broadcast_to([P, TOK, E])
            per_expert = lambda ap: ap.unsqueeze(1).broadcast_to([P, TOK, E])

            def pick(s, k1, k3, ks):
                r2 = per_tok(rr[:, k3 % 2, 0:TOK])
                tt, ttr = dve.tensor_tensor, dve.tensor_reduce
                o1, o2 = oo[:, 0, :, :], oo[:, 1, :, :]
                for k in ks:
                    if k == 1:
                        dve.wait_ge(rstd_ready, s + 4)
                    else:
                        dve.wait_ge(pick_step, (s + 1) * PICK_OPS + k - 1)
                    if k == 1:
                        ins = tt(lo[:, :, :], lg[:, k1 % 2, :, :], r2, ALU.mult)
                    elif k == 2:
                        ins = tt(lo[:, :, :], lo[:, :, :], per_expert(router_bias[:, :]), ALU.add)
                    elif k == 3:
                        ins = ttr(m1[:, :], lo[:, :, :], AX.X, ALU.max)
                    elif k == 4:
                        ins = tt(o1, lo[:, :, :], per_tok(m1[:, :]), ALU.is_equal)
                    elif k == 5:
                        ins = tt(o1, o1, per_expert(order[:, :]), ALU.mult)
                    elif k == 6:
                        ins = ttr(pm[:, :], o1, AX.X, ALU.max)
                    elif k == 7:
                        ins = tt(o1, o1, per_tok(pm[:, :]), ALU.is_equal)
                    elif k == 8:
                        ins = dve.scalar_tensor_tensor(lo[:, :, :], o1, -BIG, lo[:, :, :], ALU.mult, ALU.add)
                    elif k == 9:
                        ins = ttr(m2[:, :], lo[:, :, :], AX.X, ALU.max)
                    elif k == 10:
                        ins = tt(dd[:, :], m1[:, :], m2[:, :], ALU.subtract)
                    elif k == 11:
                        ins = tt(o2, lo[:, :, :], per_tok(m2[:, :]), ALU.is_equal)
                    elif k == 12:
                        ins = tt(o2, o2, per_expert(order[:, :]), ALU.mult)
                    elif k == 13:
                        ins = ttr(pm[:, :], o2, AX.X, ALU.max)
                    elif k == 14:
                        ins = tt(o2, o2, per_tok(pm[:, :]), ALU.is_equal)
                    elif k == 15:
                        dve.wait_ge(soft_ready, s + 2)
                        ins = tt(oo[:, :, :, :], oo[:, :, :, :], ws[:, :, :].unsqueeze(3).broadcast_to([P, 2, TOK, E]), ALU.mult)
                    elif k == 16:
                        ins = tt(gg[:, :, 1, :], o1, o2, ALU.add)
                    elif k == 17:
                        ins = tt(gg[:, :, 0, :], gg[:, :, 1, :], r2, ALU.mult)
                    elif k == 18:
                        if after(s, 0):
                            dve.wait_ge(pack_turned, s * 2 + 2)
                        ins = dve.tensor_copy(pk[:, :, :, 0, :], gg[:, :, :, :])
                    else:
                        ins = tt(pk[:, :, :, 1, :], gg[:, :, :, :], pk[:, :, :, 0, :].bitcast(F32), ALU.subtract)
                    ins.then_inc(pick_step, 1)

            def scale(m, u, ku):
                dve.wait_ge(bcast_ready, u * TILES + m + 1)
                if m == 0:
                    dve.wait_ge(dup_ready, u + 1)
                if after(u, 1) or m >= NZ:
                    dve.wait_ge(expert_done, u * EP + m // 2 - 1)
                dve.tensor_tensor(zb[:, m % NZ, :], ring[:, bcast_bank(ku % 2, m), :], x2d[:, ku % 2, m % 2, :], ALU.mult)\
                   .then_inc(z_dve, 1)

            def total(u, ku):
                dve.wait_ge(expert_done, u * EP + EP)
                dve.tensor_tensor(x2t[:, ku % X2, :], b_m[:, :], x2t[:, ku % X2, :], ALU.add).then_inc(sum_done, 1)

            def gated(v):
                dve.wait_ge(gate_ready, v + 1)
                dve.wait_ge(og_ready, v + 1)
                dve.tensor_tensor(sig_c[:, :], b_t[:, :], sig_c[:, :], ALU.mult).then_inc(om_done, 1)

            def residual(v, kv):
                dve.wait_ge(om_done, v + 1)
                if after(v, X2):
                    dve.wait_ge(y_turned, v - X2 + 1)
                dve.tensor_tensor(x2t[:, kv % X2, :], b_x[:, :], sig_c[:, :], ALU.add).then_inc(x2_ready, 1)

            def back(w, kw, between=lambda n: None):
                dve.wait_ge(back_ready, w + 1)
                h, b = kw % 2, kw // 2 % 2
                for j in range(JP):
                    dve.bn_stats(bst_x[:, b, h * JP + j, :],
                                 b_d[:, j // 2, j % 2 * BACK:j % 2 * BACK + P].rearrange("p (t c) -> p c t", t=2))
                    between(j)
                logits = b_d[:, :, 0:2 * BACK].rearrange("p z (j n) -> p z j n", j=2)[:, :, :, P:BACK]
                dve.tensor_copy(lg[:, b, h * UNIT_J:(h + 1) * UNIT_J, :].rearrange("p (z j t) e -> p z j (t e)", z=2, j=2),
                                logits).then_inc(back_done, 1)

            def slot(u, ku):
                h, v = ku % 2, u + 4
                s, k = (u - h) // 2, (ku - h) // 2
                step_rstd = not isinstance(s, int) or s + 1 < STEPS
                step_pick = not isinstance(s, int) or -1 <= s < STEPS - 1
                stats = h == 1 and (not isinstance(s, int) or s + 4 < STEPS)

                def rstd(*ks):
                    if step_rstd and h == 0:
                        rstd_c(s, k + 3, ks)

                def route(even, odd):
                    if step_pick:
                        pick(s, k + 1, k + 3, odd if h else even)

                def bn(*js):
                    if stats:
                        stats_t(s + 4, js)

                if has(u - 1):
                    total(u - 1, ku - 1)
                route((), (6,))
                if has(u + 3):
                    back(u + 3, ku + 3, lambda n: route((), (7 + n,)))
                else:
                    route((), range(7, 11))
                rstd(0, 1, 2)
                route((), (11,))
                if has(u):
                    scale(2, u, ku)
                rstd(3, 4)
                route((), (12,))
                bn(0)
                rstd(5)
                route((), (13,))
                bn(1)
                route((), (14,))
                if has(u):
                    scale(4, u, ku)
                rstd(6)
                bn(2)
                rstd(7)
                route((), (15,))
                bn(3)
                rstd(8)
                if has(u):
                    scale(6, u, ku)
                rstd(9)
                route((), (16,))
                if has(u):
                    scale(7, u, ku)
                rstd(10, 11)
                route((), (17,))
                bn(4)
                rstd(12)
                route((), (18,))
                bn(5)
                rstd(13)
                if has(v):
                    gated(v)
                route((1,), (19,))
                if has(v):
                    residual(v, ku + 4)
                route((2, 3), ())
                bn(6)
                route((4,), ())
                bn(7)
                if has(u + 1):
                    scale(0, u + 1, ku + 1)
                route((5,), ())

            stats_t(0, range(8))
            rstd_c(-3, 0, range(RSTD_OPS))
            stats_t(1, range(8))
            for u in range(-4, 2 * HEAD):
                slot(u, u)
            with dve.Fori(0, LOOPS) as i:
                for k in range(2 * HEAD, 2 * (HEAD + CYCLE)):
                    slot(i * (2 * CYCLE) + k, k)
            for u in range(2 * TAIL, UNITS + 1):
                slot(u, u)


_CONV = ["ln_in_w", "ln_in_b", "ln_c_w", "ln_c_b"] + [p + s for p in PROJ for s in ("_w", "_b")]


def kernel(**inputs):
    import numpy as _np
    import concourse.bacc as _bacc
    from concourse.bass_utils import run_bass_kernel_spmd as _run

    nc = _bacc.Bacc("TRN2", target_bir_lowering=False, num_devices=1)
    arrays, aps = {}, {}
    for name, value in inputs.items():
        a = _np.ascontiguousarray(value)
        arrays[f"in_{name}"] = a
        aps[name] = nc.dram_tensor(f"in_{name}", a.shape, mybir.dt.from_np(a.dtype), kind="ExternalInput").ap()
    out = nc.dram_tensor("out_0", (1, N, N, C), F32, kind="ExternalOutput").ap()
    metaformer_kernel(nc, aps["x"], aps["L0_conv_mask"], {n: aps["L0_conv_" + n] for n in _CONV},
                      aps["L0_ffn_router_w"], aps["L0_ffn_router_b"], aps["L0_ffn_expert_w"], aps["L0_ffn_expert_b"], out)
    return _run(nc, [arrays], core_ids=[0]).results[0]["out_0"]
```

```python
from contextlib import ExitStack

import concourse.bass as bass
from concourse import mybir

F32 = mybir.dt.float32
F32R = mybir.dt.float32r
I32 = mybir.dt.int32
ALU = mybir.AluOpType
ACT = mybir.ActivationFunctionType
AX = mybir.AxisListType

P = 128
N = 256
C = 64
E = 8
Q = 2
ROWS = 16
BLOCKS = N // ROWS
GROUP = 2
ROW_RING = 4
GROUPS = ROWS // GROUP
BN_ROWS = 3
HIGH_AFTER = (1, 2)
CHUNK = 8
CHUNKS = C // CHUNK
RUN = CHUNK * ROWS
UNIT_J = 8
STEP_J = 2 * UNIT_J
STEPS = 2 * N // STEP_J
JP = UNIT_J // 2
WIDE = JP * P
CYCLE = 6
HEAD = 4
LOOPS = (STEPS - 2 * HEAD) // CYCLE
TAIL = HEAD + LOOPS * CYCLE
TOK = STEP_J
ROUTE = 4 * E
EP = E // 2
TILES = 2 * EP
POOL_TILES = [(1, 3, 5), (1, 3, 5, 7)]
DVE_TILES = [tuple(m for m in range(TILES) if m not in pool) for pool in POOL_TILES]
NZ = 4
UNITS = 2 * STEPS
X2 = 6
XC = 3
EPS_LN = 1e-5
EPS_OUTER = 1e-6
SEED = float(0x5F3759DF)
BIG = 3e38
PROJ = ["left_proj", "right_proj", "left_gate", "right_gate", "gating", "out_proj"]
LRG = 4 * C
RSTD_OPS = 14
PICK_OPS = 19
STAT_OPS_A = 13
BACK = P + 2 * E
EARLY = {n: [] for n in range(BLOCKS)}
EARLY.update({10: [(0, 0, 6)], 11: [(0, 6, 10)], 12: [(1, 0, 6)], 13: [(0, 10, 13), (1, 6, 12)], 14: [(0, 13, 14), (1, 12, 13)]})
PARTS = [1 + sum(c == b for early in EARLY.values() for c, _, _ in early) for b in range(2)]
RING_USES = [[("bcast", m) for m in range(2, TILES)] + [("y", 0)] + pack + [("bcast", 0), ("bcast", 1)]
             for pack in ([], [("pack", 0), ("pack", 1)])]


def ring_bank(h, kind, m):
    return (h * len(RING_USES[0]) + RING_USES[h].index((kind, m))) % 2


def bcast_bank(h, m):
    return ring_bank(1 - h if m < 2 else h, "bcast", m)


def y_bank(h):
    return ring_bank(1 - h, "y", 0)


def pack_bank(w):
    return ring_bank(1, "pack", w)


def tiles_before(tiles, u, ku, m=0, more=0):
    h = ku % 2
    step = len(tiles[0] + tiles[1])
    return (u - h - 2) // 2 * step + (step + (len(tiles[0]) if h else 0) + sum(t < m for t in tiles[h]) + more)


def after(n, k):
    return not isinstance(n, int) or n >= k


def has(u):
    return not isinstance(u, int) or 0 <= u < UNITS


def metaformer_kernel(nc, x, mask, weights, router_w, router_b, expert_w, expert_b, out):
    lr_dram = nc.dram_tensor("left_right_scratch", [BLOCKS, P, Q * 2 * C * ROWS], F32, kind="Internal").ap()
    x_rows = x.rearrange("a (b r) (p q) c -> (a b) p r (q c)", r=ROWS, q=Q)
    x_units = x.rearrange("a (h p) (u j) c -> (a h) u p j c", p=P, j=UNIT_J)
    out_units = out.rearrange("a (h p) (u j) c -> (a h) u p j c", p=P, j=UNIT_J)
    HALF = UNITS // 2

    with ExitStack() as ctx:
        def sem(name):
            return ctx.enter_context(nc.semaphore(name))

        def keep(name, shape, dt=F32):
            return ctx.enter_context(nc.sbuf_tensor(name, shape, dt))

        turn_route = keep("turn_route", [P, BACK])
        ident = turn_route[:, 0:P]
        w_router = turn_route[:, P:BACK]
        w_exp = keep("w_exp", [P, EP, C])
        w_og = keep("w_og", [P, 2, P])
        bias_hi = keep("bias_hi", [P, 2, P], F32R)
        bias_lo = keep("bias_lo", [P, 2, P], F32R)
        router_bias = keep("router_bias", [P, E])
        order = keep("order", [P, E])
        rx = keep("rx", [P, 2 * N])
        bx = keep("bx", [P, 2 * N])

        def layer(tensors, psums=()):
            made = []
            with ExitStack() as c:
                for name, shape, *dt in tensors:
                    made.append(c.enter_context(nc.sbuf_tensor(name, shape, *(dt or [F32]))))
                for name, shape in psums:
                    made.append(c.enter_context(nc.psum_tensor(name, shape, F32)))
            return made

        (w_nat, ln_col, bias_row, w_diff, ones, e_nat, r_nat, eb_wide, mask_in) = layer([
            ("w_nat", [C, 6, 2, C]), ("ln_col", [P, 4]), ("bias_row", [1, 6 * C]), ("w_diff", [P, 6 * C]),
            ("ones", [P, P]), ("e_nat", [P, E, C]), ("r_nat", [P, E]), ("eb_wide", [P, 2, P]),
            ("mask_in", [P, 2, N])])
        setup_bytes = 4 * (12 * C + 4 + 6 * C + 6 * C + P + E * C + E + 2 * P + 2 * N)
        (_, w_proj, w_hi, w_lo, mt, r_all, b_all, xa, xh, xs, xts, sig_a, stage, bst, nv, ny, nt) = layer([
            ("skip_setup", [P, setup_bytes // 4 + 128]),
            ("w_proj", [P, 6 * C]),
            ("w_hi", [P, LRG], F32R),
            ("w_lo", [P, LRG], F32R),
            ("mt", [P, N, Q]), ("r_all", [P, N, Q]), ("b_all", [P, N, Q]),
            ("xa", [P, 2, ROWS, Q * C]), ("xh", [P, ROWS, Q * C]),
            ("xs", [P, 2, ROWS, Q, 2, C], F32R),
            ("xts", [P, 2, GROUP * Q * P], F32R),
            ("sig_a", [P, ROW_RING, Q, 2 * C]), ("stage", [P, 2, Q, 2 * CHUNKS, ROWS, CHUNK]),
            ("bst", [P, ROWS, 6]), ("nv", [P, ROWS * Q]), ("ny", [P, ROWS * Q]), ("nt", [P, ROWS * Q])])
        (ps_set,) = layer([], [("ps_set", [P, 8, 512])])
        (xt_a, pr_a) = layer([], [("xt_a", [P, 2, 512]), ("pr_a", [P, ROW_RING, Q * LRG])])

        (t_all, chunk) = layer([("t_all", [P, C, 2 * N]), ("chunk", [P, 2, 2 * Q, BLOCKS, RUN])])
        (ein,) = layer([], [("ein", [P, 4, 512])])

        (_, sel, xc, xn, tn, ttn, xtn, sig_c, x2t, x2d, zb, bcs, wt, outc, bst_t, bst_x, v32, y32, t32, rr, bt, lg, lo, gg,
         oo, ws, pk) = layer([
            ("t_keep", [P, C, 2 * N]),
            ("sel", [P, 2, 2, E, C], F32R),
            ("xc", [P, XC, UNIT_J, C]), ("xn", [P, UNIT_J, C]), ("tn", [P, UNIT_J, C]),
            ("ttn", [P, WIDE]), ("xtn", [P, WIDE]), ("sig_c", [P, WIDE]), ("x2t", [P, X2, WIDE]), ("x2d", [P, 2, 2, WIDE]),
            ("zb", [P, NZ, WIDE]), ("bcs", [P, 2, WIDE]), ("wt", [P, 2, 2, WIDE // 2], F32R),
            ("outc", [P, 2, UNIT_J, C]), ("bst_t", [P, 2, TOK // 2, 6]), ("bst_x", [P, 2, TOK // 2, 6]),
            ("v32", [P, 2 * TOK]), ("y32", [P, 2 * TOK]), ("t32", [P, 2 * TOK]), ("rr", [P, 2, 2 * TOK]),
            ("bt", [P, 2, TOK]), ("lg", [P, 2, TOK, E]), ("lo", [P, TOK, E]), ("gg", [P, TOK, 2, E]),
            ("oo", [P, 2, TOK, E]), ("ws", [P, 2, TOK]), ("pk", [P, TOK, 2, 2, E], F32R)])
        m1, m2, pm, dd = v32[:, 0:TOK], v32[:, TOK:2 * TOK], y32[:, 0:TOK], y32[:, TOK:2 * TOK]
        (b_t, b_g, b_x, b_d, b_m, ring) = layer([], [
            ("b_t", [P, 512]), ("b_g", [P, 512]), ("b_x", [P, 512]), ("b_d", [P, 2, 512]),
            ("b_m", [P, 512]), ("ring", [P, 2, 512])])

        set_step = sem("set_step"); w_in = sem("w_in"); const_in = sem("const_in")
        id_made = sem("id_made"); pool_const = sem("pool_const")
        set_pe = sem("set_pe"); set_dve = sem("set_dve"); set_act = sem("set_act")
        x_in = [sem("x_in0"), sem("x_in1")]
        stats_ready = sem("stats_ready"); stat_step = sem("stat_step")
        xh_step = sem("xh_step"); xh_done = sem("xh_done"); hi_ready = sem("hi_ready"); xh_ready = sem("xh_ready")
        xt_ready = sem("xt_ready"); xts_ready = sem("xts_ready"); proj_ready = sem("proj_ready")
        sig_ready = sem("sig_ready"); lr_done = sem("lr_done"); stored = [sem("stored0"), sem("stored1")]
        turn_ready = sem("turn_ready"); turned = sem("turned")
        chunk_in = [sem("chunk_in0"), sem("chunk_in1")]
        ein_ready = sem("ein_ready"); ein_act = sem("ein_act"); ein_dve = sem("ein_dve")
        xc_in = [sem("xc_in0"), sem("xc_in1"), sem("xc_in2")]; sel_made = sem("sel_made")
        rstd_step = sem("rstd_step"); rstd_ready = sem("rstd_ready"); bn_t_done = sem("bn_t_done")
        norm_step = sem("norm_step"); x_norm = sem("x_norm"); norm_ready = sem("norm_ready")
        turns_ready = sem("turns_ready"); turns_out = sem("turns_out"); g_ready = sem("g_ready"); og_ready = sem("og_ready")
        dup_ready = sem("dup_ready")
        gate_ready = sem("gate_ready"); om_done = sem("om_done"); x2_ready = sem("x2_ready")
        back_ready = sem("back_ready"); back_done = sem("back_done")
        pick_step = sem("pick_step"); soft_ready = sem("soft_ready")
        pack_turned = sem("pack_turned"); pack_out = sem("pack_out")
        bcast_ready = sem("bcast_ready"); bcast_out = sem("bcast_out")
        z_dve = sem("z_dve"); z_pool = sem("z_pool"); expert_done = sem("expert_done")
        sum_done = sem("sum_done"); y_turned = sem("y_turned"); y_out = sem("y_out")
        out_stored = [sem("out_stored0"), sem("out_stored1")]

        block = ctx.enter_context(nc.Block())
        NW, NC = 17, 8
        NX = 4

        @block.sync
        def _(sp):
            twice = lambda ap: ap.unsqueeze(0).broadcast_to([2] + list(ap.shape))

            def load_x(n, b):
                if after(n, 2):
                    sp.wait_ge(xh_done, (n - 1) * 2)
                sp.dma_start(xa[:, b, :, :], x_rows[n]).then_inc(x_in[b], 16)

            def block_a(n, b, last=False):
                if not last:
                    load_x(n + 3, 1 - b)
                sp.wait_ge(lr_done, (n + 1) * ROWS)
                sp.dma_start(lr_dram[n], stage[:, b, :, :, :, :].rearrange("p q s r c -> p (q s r c)")).then_inc(stored[b], 16)

            def load_blocks(c, b, blocks):
                for u in range(2 * Q):
                    part = lr_dram.rearrange("n p (u c) -> u p n c", u=2 * Q)[u, :, blocks, c * RUN:(c + 1) * RUN]
                    sp.dma_start(chunk[:, b, u, blocks, :], part).then_inc(chunk_in[b], 16)

            def direct():
                for u in range(2 * Q):
                    sp.dma_start(chunk[:, 0, u, BLOCKS - 2:BLOCKS, :],
                                 stage[:, :, u // 2, u % 2 * CHUNKS, :, :].rearrange("p b r c -> p b (r c)")).then_inc(chunk_in[0], 16)

            load_x(0, 0)
            for k, name in enumerate(PROJ):
                sp.dma_start(w_nat[:, k, :, :], weights[name + "_w"].unsqueeze(1).broadcast_to([C, 2, C])).then_inc(w_in, 16)
            for col, name in enumerate(["ln_in_w", "ln_in_b", "ln_c_w", "ln_c_b"]):
                sp.dma_start(ln_col[:, col:col + 1], twice(weights[name].rearrange("(c a) -> c a", a=1))).then_inc(w_in, 16)
            for k, name in enumerate(PROJ):
                sp.dma_start(bias_row[:, k * C:(k + 1) * C],
                             weights[name + "_b"].rearrange("(a c) -> a c", a=1)).then_inc(w_in, 16)
            sp.dma_start(mask_in[:, :, :], mask.rearrange("a (h p) k -> p (a h) k", p=P)).then_inc(w_in, 16)
            load_x(1, 1)
            for half in range(2):
                sp.dma_start(e_nat[half * C:half * C + C, :, :], expert_w.rearrange("e d c -> d e c")).then_inc(const_in, 16)
            sp.dma_start(r_nat[:, :], twice(router_w)).then_inc(const_in, 16)
            sp.dma_start(router_bias[:, :], router_b.rearrange("(a e) -> a e", a=1).broadcast_to([P, E])).then_inc(const_in, 16)
            sp.wait_ge(pool_const, 3)
            for t in range(4):
                row, half = t * ROUTE + 2 * E, t % 2
                sp.dma_start(eb_wide[row:row + 2 * E, t // 2, half * C:half * C + C], twice(expert_b)).then_inc(const_in, 16)

            load_x(2, 0)
            for n in range(BLOCKS):
                if n == BLOCKS - 1:
                    sp.wait_ge(lr_done, BLOCKS * ROWS)
                    direct()
                block_a(n, n % 2, n + 3 >= BLOCKS)
                for c, first, end in EARLY[n]:
                    sp.wait_ge(stored[0], 16 * ((end + 1) // 2))
                    sp.wait_ge(stored[1], 16 * (end // 2))
                    load_blocks(c, c, slice(first, end))

            for b in range(2):
                sp.wait_ge(stored[b], 16 * BLOCKS // 2)
            load_blocks(1, 1, slice(BLOCKS - 3, BLOCKS))
            for c in range(2, CHUNKS):
                sp.wait_ge(ein_ready, (c - 1) * CHUNK)
                load_blocks(c, c % 2, slice(0, BLOCKS))
            sp.wait_ge(ein_ready, C)

            def load_unit(v, kv):
                if after(v, XC):
                    sp.wait_ge(turns_ready, v - XC + 1)
                sp.dma_start(xc[:, kv % XC, :, :], x_units[v // HALF, v % HALF]).then_inc(xc_in[kv % XC], 16)

            def store_unit(u, ku):
                sp.wait_ge(y_out, u + 1)
                sp.dma_start(out_units[u // HALF, u % HALF], outc[:, ku % 2, :, :]).then_inc(out_stored[ku % 2], 16)

            def slot(u, ku):
                if has(u + 6):
                    load_unit(u + 6, ku + 6)
                if has(u - 1):
                    store_unit(u - 1, ku - 1)

            for v in range(XC):
                load_unit(v, v)
            for u in range(XC - 6, 2 * HEAD):
                slot(u, u)
            with sp.Fori(0, LOOPS) as i:
                for k in range(2 * HEAD, 2 * (HEAD + CYCLE)):
                    slot(i * (2 * CYCLE) + k, k)
            for u in range(2 * TAIL, UNITS + 1):
                slot(u, u)
            for h in range(2):
                sp.wait_ge(out_stored[h], 16 * UNITS // 2)

        @block.gpsimd
        def _(pool):
            pool.memset(ident[:, :], 0.0).then_inc(id_made, 1)
            pool.memset(ones[:, :], 1.0 / C).then_inc(pool_const, 1)
            pool.memset(w_router, 0.0).then_inc(pool_const, 1)
            pool.memset(eb_wide[:, :, :], 0.0).then_inc(pool_const, 1)
            pool.memset(w_og[:, :, :], 0.0).then_inc(pool_const, 1)
            for e in range(E):
                m = pool.memset(order[:, e:e + 1], float(E - e))
            m.then_inc(pool_const, 1)
            pool.wait_ge(id_made, 1)
            pool.affine_select(out=ident[:, :], in_=ident[:, :], compare_op=ALU.not_equal, fill=1.0, base=0,
                               pattern=[[-1, P]], channel_multiplier=1).then_inc(id_made, 1)

            def block_a(n, b):
                halves = [slice(0, ROWS // 2), slice(ROWS // 2, ROWS)]

                def per_token(ap, half):
                    return ap[:, bass.ds(n * ROWS + half.start, ROWS // 2), :].rearrange("p r q -> p (r q)")\
                        .unsqueeze(2).broadcast_to([P, ROWS // 2 * Q, C])

                tokens = lambda ap: ap.rearrange("p r (q c) -> p (r q) c", q=Q)
                pool.wait_ge(stats_ready, n + 1)
                if after(n, 1):
                    pool.wait_ge(xh_ready, n)
                for half in halves:
                    pool.tensor_tensor(tokens(xh[:, half, :]), tokens(xa[:, b, half, :]), per_token(r_all, half), ALU.mult)\
                        .then_inc(xh_step, 1)
                for h, half in enumerate(halves):
                    pool.wait_ge(xh_step, n * 2 + h + 1)
                    pool.tensor_tensor(tokens(xh[:, half, :]), tokens(xh[:, half, :]), per_token(b_all, half), ALU.add)\
                        .then_inc(xh_done, 1)
                for h, half in enumerate(halves):
                    pool.wait_ge(hi_ready, n * 2 + h + 1)
                    ins = pool.tensor_tensor(
                        xs[:, b, half, :, 1, :].rearrange("p r q c -> p (r q) c"), tokens(xh[:, half, :]),
                        xs[:, b, half, :, 0, :].bitcast(F32).rearrange("p r q c -> p (r q) c"), ALU.subtract)
                ins.then_inc(xh_ready, 1)

            block_a(0, 0)
            block_a(1, 1)
            with pool.Fori(1, BLOCKS // 2) as i:
                block_a(i * 2, 0)
                block_a(i * 2 + 1, 1)

            def norm(v, kv, between=lambda: None):
                pool.wait_ge(xc_in[kv % XC], (v - kv % XC) // XC * 16 + 16)
                h, b = kv % 2, kv // 2 % 2
                s = (v - h) // 2
                pool.wait_ge(rstd_ready, s + 1)
                if after(v, 1):
                    pool.wait_ge(turns_ready, v)
                cols = slice(h * UNIT_J, h * UNIT_J + UNIT_J)
                t_in = t_all[:, :, bass.ts(v, UNIT_J)].rearrange("p c j -> p j c")
                r_t = rr[:, b, TOK + h * UNIT_J:TOK + (h + 1) * UNIT_J].unsqueeze(2).broadcast_to([P, UNIT_J, C])
                b_tt = bt[:, b, cols].unsqueeze(2).broadcast_to([P, UNIT_J, C])
                r_x = rx[:, bass.ts(v, UNIT_J)].unsqueeze(2).broadcast_to([P, UNIT_J, C])
                b_xx = bx[:, bass.ts(v, UNIT_J)].unsqueeze(2).broadcast_to([P, UNIT_J, C])
                first = isinstance(v, int) and v < NX
                steps = v if first else v * 2 - NX
                if not first:
                    pool.tensor_tensor(xn[:, :, :], xc[:, kv % XC, :, :], r_x, ALU.mult).then_inc(norm_step, 1)
                pool.tensor_tensor(tn[:, :, :], t_in, r_t, ALU.mult).then_inc(norm_step, 1)
                between()
                if not first:
                    pool.wait_ge(norm_step, steps + 1)
                    pool.tensor_tensor(xn[:, :, :], xn[:, :, :], b_xx, ALU.add)
                pool.wait_ge(norm_step, steps + (1 if first else 2))
                pool.tensor_tensor(tn[:, :, :], tn[:, :, :], b_tt, ALU.add).then_inc(norm_ready, 1)

            def scale(m, u, ku):
                pool.wait_ge(bcast_out, tiles_before(POOL_TILES, u, ku, m) + 1)
                if m == 1:
                    pool.wait_ge(dup_ready, u + 1)
                if after(u, 1) or m >= NZ:
                    pool.wait_ge(expert_done, u * EP + m // 2 - 1)
                pool.tensor_tensor(zb[:, m % NZ, :], bcs[:, tiles_before(POOL_TILES, ku, ku, m) % 2, :], x2d[:, ku % 2, m % 2, :], ALU.mult)\
                    .then_inc(z_pool, 1)

            def slot(u, ku):
                if has(u):
                    scale(3, u, ku)

                def later():
                    for m in POOL_TILES[ku % 2][2:]:
                        if has(u):
                            scale(m, u, ku)

                if has(u + 5):
                    norm(u + 5, ku + 5, later)
                else:
                    later()
                if has(u + 1):
                    scale(1, u + 1, ku + 1)

            pool.wait_ge(ein_ready, (CHUNKS - 1) * CHUNK)
            kinds = ident[:, :].rearrange("p (t k e) -> p t k e", t=4, k=4)
            for t in range(4):
                ins = pool.tensor_tensor(sel[:, t // 2, t % 2, :, :],
                                         kinds[:, t, 0, :].unsqueeze(2).broadcast_to([P, E, C]),
                                         kinds[:, t, 1, :].unsqueeze(2).broadcast_to([P, E, C]), ALU.add)
            ins.then_inc(sel_made, 1)
            pool.wait_ge(ein_ready, C)
            norm(0, 0)
            for u in range(-4, 2 * HEAD):
                slot(u, u)
            with pool.Fori(0, LOOPS) as i:
                for k in range(2 * HEAD, 2 * (HEAD + CYCLE)):
                    slot(i * (2 * CYCLE) + k, k)
            for u in range(2 * TAIL, UNITS):
                slot(u, u)

        @block.scalar
        def _(act):
            act.wait_ge(set_pe, 2)
            for h in range(2):
                for q in range(Q):
                    ins = act.activation(mt[:, h * P:h * P + P, q], ps_set[:, 1, (2 * h + q) * P:(2 * h + q + 1) * P], ACT.Copy)
            ins.then_inc(set_act, 1)

            def high(n, b, h):
                half = slice(h * ROWS // 2, (h + 1) * ROWS // 2)
                act.wait_ge(xh_done, n * 2 + h + 1)
                if h == 0 and after(n, 2):
                    act.wait_ge(xt_ready, (n - 1) * GROUPS)
                act.activation(xs[:, b, half, :, 0, :].rearrange("p r q c -> p (r q) c"),
                               xh[:, half, :].rearrange("p r (q c) -> p (r q) c", q=Q), ACT.Copy).then_inc(hi_ready, 1)

            def evacuate(n, g, b):
                act.wait_ge(xt_ready, n * GROUPS + g + 1)
                if after(n, 1) or g >= 2:
                    act.wait_ge(proj_ready, (n * GROUPS + g - 1) * GROUP)
                act.activation(xts[:, g % 2, :], xt_a[:, g % 2, :], ACT.Copy).then_inc(xts_ready, 1)

            def gates(n, g):
                for r in range(GROUP):
                    k = (g * GROUP + r) % ROW_RING
                    act.wait_ge(proj_ready, (n * GROUPS + g) * GROUP + r + 1)
                    act.activation(sig_a[:, k, :, :], pr_a[:, k, :].rearrange("p (q c) -> p q c", q=Q)[:, :, 2 * C:4 * C],
                                   ACT.Sigmoid).then_inc(sig_ready, 1)

            def block_a(n, b, last=False):
                for g in range(GROUPS):
                    if g < GROUPS - 1:
                        evacuate(n, g + 1, b)
                    elif not last:
                        evacuate(n + 1, 0, b)
                    gates(n, g)
                    if g in HIGH_AFTER and not last:
                        high(n + 1, 1 - b, HIGH_AFTER.index(g))

            high(0, 0, 0)
            high(0, 0, 1)
            evacuate(0, 0, 0)
            block_a(0, 0)
            block_a(1, 1)
            with act.Fori(1, BLOCKS // 2 - 1) as i:
                block_a(i * 2, 0)
                block_a(i * 2 + 1, 1)
            block_a(BLOCKS - 2, 0)
            block_a(BLOCKS - 1, 1, True)
            act.wait_ge(turn_ready, 1)
            for k, dst in enumerate([rx, bx]):
                for h in range(2):
                    for q in range(Q):
                        ins = act.activation(dst[:, h * N:h * N + N].rearrange("p (j q) -> p j q", q=Q)[:, :, q],
                                             pr_a[:, k, (2 * h + q) * P:(2 * h + q + 1) * P], ACT.Copy)
            ins.then_inc(turned, 1)

            act.wait_ge(set_dve, 4)
            def chunk_b(c):
                for k in range(0, CHUNK, 2):
                    act.wait_ge(ein_ready, c * CHUNK + k + 1)
                    act.activation(t_all[:, bass.ds(c * CHUNK + k, 1), :].rearrange("p a n -> p (a n)"),
                                   ein[:, k % 4, :], ACT.Copy).then_inc(ein_act, 1)

            with act.Fori(0, CHUNKS) as c:
                chunk_b(c)

            def front(v):
                act.wait_ge(turns_ready, v + 1)
                if after(v, 1):
                    act.wait_ge(og_ready, v)
                act.activation(xtn[:, :], b_g[:, :], ACT.Copy)
                act.activation(ttn[:, :], b_t[:, :], ACT.Copy).then_inc(turns_out, 1)

            def gate(v):
                act.wait_ge(g_ready, v + 1)
                if after(v, 1):
                    act.wait_ge(x2_ready, v)
                act.activation(sig_c[:, :], b_g[:, :], ACT.Sigmoid).then_inc(gate_ready, 1)

            def double(w, kw, t):
                if t == 0:
                    act.wait_ge(x2_ready, w + 1)
                    if after(w, 2):
                        act.wait_ge(z_dve, tiles_before(DVE_TILES, w - 1, kw - 1))
                        act.wait_ge(z_pool, tiles_before(POOL_TILES, w - 1, kw - 1))
                for half in range(2):
                    ins = act.activation(x2d[half * C:(half + 1) * C, kw % 2, t, :], x2t[t * C:(t + 1) * C, kw % X2, :], ACT.Copy)
                if t == 1:
                    ins.then_inc(dup_ready, 1)

            def y_evacuate(u, ku):
                act.wait_ge(y_turned, u + 1)
                h = ku % 2
                if after(u, 2):
                    act.wait_ge(out_stored[h], (u - h) * 8)
                act.activation(outc[:, h, :, :].rearrange("p j c -> p (j c)"), ring[:, y_bank(h), :], ACT.Copy)\
                   .then_inc(y_out, 1)

            def bcast(m, u, ku):
                act.wait_ge(bcast_ready, u * TILES + m + 1)
                if after(u, 1) or m >= 5:
                    act.wait_ge(z_pool, tiles_before(POOL_TILES, u, ku, m, -1))
                act.activation(bcs[:, tiles_before(POOL_TILES, ku, ku, m) % 2, :], ring[:, bcast_bank(ku % 2, m), :], ACT.Copy).then_inc(bcast_out, 1)

            def soft(s):
                act.wait_ge(pick_step, (s + 1) * PICK_OPS + 10)
                act.activation(ws[:, 0, :], dd[:, :], ACT.Sigmoid)
                act.activation(ws[:, 1, :], dd[:, :], ACT.Sigmoid, scale=-1.0).then_inc(soft_ready, 1)

            def pack(w, kw):
                act.wait_ge(pack_turned, w + 1)
                act.activation(wt[:, kw // 2 % 2, kw % 2, :], ring[:, pack_bank(kw % 2), 0:WIDE // 2], ACT.Copy).then_inc(pack_out, 1)

            def slot(u, ku):
                odd = ku % 2 == 1
                if has(u):
                    bcast(3, u, ku)
                if has(u + 4):
                    front(u + 4)
                if odd and has(u + 1):
                    soft((u - 1) // 2)
                if has(u):
                    bcast(5, u, ku)
                if has(u + 1):
                    double(u + 1, ku + 1, 0)
                if has(u) and odd:
                    bcast(7, u, ku)
                if has(u + 1):
                    double(u + 1, ku + 1, 1)
                if has(u + 4):
                    gate(u + 4)
                if has(u - 1):
                    y_evacuate(u - 1, ku - 1)
                if odd and has(u + 1):
                    pack(u + 1, ku + 1)
                    pack(u + 2, ku + 2)
                if has(u + 1):
                    bcast(1, u + 1, ku + 1)

            for u in range(-4, 2 * HEAD):
                slot(u, u)
            with act.Fori(0, LOOPS) as i:
                for k in range(2 * HEAD, 2 * (HEAD + CYCLE)):
                    slot(i * (2 * CYCLE) + k, k)
            for u in range(2 * TAIL, UNITS + 1):
                slot(u, u)

        @block.tensor
        def _(pe):
            pe.wait_ge(id_made, 2)
            pe.wait_ge(w_in, 16 * NW)
            for k in range(6):
                m = pe.transpose(ps_set[:, 0, k * C:(k + 1) * C], w_nat[:, k, :, :].rearrange("p a c -> p (a c)"), ident[0:C, 0:C])
            m.then_inc(set_pe, 1)
            for h in range(2):
                for q in range(Q):
                    m = pe.transpose(ps_set[:, 1, (2 * h + q) * P:(2 * h + q + 1) * P],
                                     mask_in[:, h, :].rearrange("p (k q) -> p k q", q=Q)[:, :, q], ident[:, :])
            m.then_inc(set_pe, 1)
            pe.wait_ge(set_dve, 1)
            pe.matmul(ps_set[:, 4, 0:6 * C], ones[0:C, :], w_diff[0:C, :], start=True, stop=False)
            pe.matmul(ps_set[:, 4, 0:6 * C], ones[0:1, :], bias_row[:, :], start=False, stop=True).then_inc(set_pe, 1)
            pe.wait_ge(set_dve, 3)
            pe.wait_ge(set_act, 1)

            def turn(n, g, b):
                pe.wait_ge(xh_ready, n + 1)
                if after(n, 1) or g >= 2:
                    pe.wait_ge(xts_ready, n * GROUPS + g - 1)
                for r in range(GROUP):
                    for q in range(Q):
                        m = pe.transpose(xt_a[:, g % 2, (r * Q + q) * P:(r * Q + q + 1) * P],
                                         xs[:, b, g * GROUP + r, q, :, :].bitcast(F32).rearrange("p z c -> p (z c)"), ident)
                m.then_inc(xt_ready, 1)

            def project(n, g):
                pe.wait_ge(xts_ready, n * GROUPS + g + 1)
                for r in range(GROUP):
                    k = (g * GROUP + r) % ROW_RING
                    if after(n, 1) or g * GROUP >= ROW_RING:
                        pe.wait_ge(lr_done, (n * GROUPS + g) * GROUP + (r + 1 - ROW_RING))
                    for q in range(Q):
                        for w in (w_hi, w_lo):
                            ins = pe.matmul(pr_a[:, k, q * LRG:(q + 1) * LRG], xts[:, g % 2, (r * Q + q) * P:(r * Q + q + 1) * P],
                                            w[:, :], start=w is w_hi, stop=w is w_lo)
                    ins.then_inc(proj_ready, 1)

            def block_a(n, b, last=False):
                for g in range(GROUPS):
                    if g < GROUPS - 1:
                        turn(n, g + 1, b)
                    elif not last:
                        turn(n + 1, 0, 1 - b)
                    project(n, g)

            turn(0, 0, 0)
            block_a(0, 0)
            block_a(1, 1)
            with pe.Fori(1, BLOCKS // 2 - 1) as i:
                block_a(i * 2, 0)
                block_a(i * 2 + 1, 1)
            block_a(BLOCKS - 2, 0)
            block_a(BLOCKS - 1, 1, True)
            pe.wait_ge(lr_done, BLOCKS * ROWS)
            for k, src in enumerate([r_all, b_all]):
                for h in range(2):
                    for q in range(Q):
                        m = pe.transpose(pr_a[:, k, (2 * h + q) * P:(2 * h + q + 1) * P],
                                         src[:, h * P:h * P + P, q], ident[:, :])
            m.then_inc(turn_ready, 1)
            pe.wait_ge(const_in, 16 * NC)
            pe.matmul(ps_set[:, 6, :], ones[0:C, :], e_nat[0:C, :, :].rearrange("p e c -> p (e c)"), start=True, stop=True)
            pe.matmul(ps_set[:, 7, 0:E], ones[0:C, :], r_nat[0:C, :], start=True, stop=True).then_inc(set_pe, 1)
            pe.wait_ge(turned, 1)

            def chunk_b(c, b):
                loads = 2 * Q * 16
                first = PARTS[b] * loads
                pe.wait_ge(chunk_in[b], c // 2 * loads + first if isinstance(c, int) else (c - b) * (loads // 2) + first)
                for k in range(CHUNK):
                    if after(c, 1) or k >= 4:
                        pe.wait_ge(ein_dve if k % 2 else ein_act, c * (CHUNK // 2) + k // 2 - 1)
                    side = chunk[:, b, :, :, :].rearrange("p u n (r c) -> p u (n r) c", c=CHUNK)[:, :, :, k]
                    for h in range(2):
                        for q in range(Q):
                            m = pe.matmul(ein[:, k % 4, h * N:h * N + N],
                                          side[:, 2 * q, h * P:h * P + P], side[:, 2 * q + 1, :], start=q == 0, stop=q == 1)
                    m.then_inc(ein_ready, 1)

            chunk_b(0, 0)
            chunk_b(1, 1)
            with pe.Fori(1, CHUNKS // 2) as i:
                chunk_b(i * 2, 0)
                chunk_b(i * 2 + 1, 1)
            pe.wait_ge(ein_act, C // 2)
            pe.wait_ge(ein_dve, C // 2)

            pe.wait_ge(sel_made, 1)

            pairs = [slice(j * P, j * P + P) for j in range(JP)]
            of_pair = lambda bank, a: bank.rearrange("p (q a i) -> p q a i", q=2, a=2)[:, :, a, :]

            def turns(v, kv):
                pe.wait_ge(norm_ready, v + 1)
                if isinstance(v, int) and v < NX:
                    pe.wait_ge(x_norm, 2 * v + 2)
                if after(v, 1):
                    pe.wait_ge(x2_ready, v)
                for dst, src in ((b_g, xn[:, :, :]), (b_t, tn[:, :, :]), (b_x, xc[:, kv % XC, :, :])):
                    for j in range(JP):
                        m = pe.transpose(dst[:, pairs[j]], src[:, 2 * j:2 * j + 2, :].rearrange("p j c -> p (j c)"), ident)
                m.then_inc(turns_ready, 1)

            def out_gate(v):
                pe.wait_ge(turns_out, v + 1)
                pe.matmul(b_g[:, :], w_og[:, 0, :], xtn[:, :], start=True, stop=True).then_inc(g_ready, 1)
                pe.matmul(b_t[:, :], w_og[:, 1, :], ttn[:, :], start=True, stop=True).then_inc(og_ready, 1)

            def back(w, kw):
                pe.wait_ge(x2_ready, w + 1)
                if after(w, 1):
                    pe.wait_ge(back_done, w)
                for j in range(JP):
                    m = pe.matmul(b_d[:, j // 2, j % 2 * BACK:(j % 2 + 1) * BACK], x2t[:, kw % X2, pairs[j]], turn_route[:, :],
                                  start=True, stop=True)
                m.then_inc(back_ready, 1)

            def ring_free(kind, m, u, h):
                r = RING_USES[h].index((kind, m))
                while True:
                    r -= 2
                    if r < 0:
                        u, h = u - 1, 1 - h
                        r += len(RING_USES[h])
                        if isinstance(u, int) and u < -1:
                            return
                    kind, m = RING_USES[h][r]
                    unit = {"bcast": u + 1 if m < 2 else u, "y": u - 1, "pack": u + 1 + m}[kind]
                    unit_h = 1 - h if m < 2 else h
                    if has(unit):
                        break
                if kind == "bcast" and m in DVE_TILES[unit_h]:
                    pe.wait_ge(z_dve, tiles_before(DVE_TILES, unit, unit_h, m) + 1)
                elif kind == "bcast":
                    pe.wait_ge(bcast_out, tiles_before(POOL_TILES, unit, unit_h, m) + 1)
                elif kind == "y":
                    pe.wait_ge(y_out, unit + 1)
                else:
                    pe.wait_ge(pack_out, unit + 1)

            def bcast(m, u, ku):
                slot_u, slot_h = (u - 1, 1 - ku % 2) if m < 2 else (u, ku % 2)
                ring_free("bcast", m, slot_u, slot_h)
                if m == 0:
                    pe.wait_ge(pack_out, u + 1)
                for a in range(2):
                    ins = pe.matmul(of_pair(ring[:, bcast_bank(ku % 2, m), :], a),
                                    sel[:, a, m % 2, m // 2 * 2:m // 2 * 2 + 2, :].rearrange("p e c -> p (e c)"),
                                    wt[:, ku // 2 % 2, ku % 2, :], start=True, stop=True)
                ins.then_inc(bcast_ready, 1)

            def bias(u, ku):
                if after(u, 1):
                    pe.wait_ge(sum_done, u)
                for a in range(2):
                    for part, b in enumerate((bias_hi, bias_lo)):
                        pe.matmul(of_pair(b_m[:, :], a), b[:, a, :], wt[:, ku // 2 % 2, ku % 2, :],
                                  start=a == 0 and part == 0, stop=False, skip_group_check=True)

            def expert(ep, u, ku):
                pe.wait_ge(z_dve, tiles_before(DVE_TILES, u, ku, 2 * ep + 2))
                pe.wait_ge(z_pool, tiles_before(POOL_TILES, u, ku, 2 * ep + 2))
                for t in range(2):
                    ins = pe.matmul(b_m[t * C:(t + 1) * C, :], w_exp[:, ep, :], zb[:, (2 * ep + t) % NZ, :], start=False,
                                    stop=ep == EP - 1, skip_group_check=True)
                ins.then_inc(expert_done, 1)

            def y_turn(u, ku):
                ring_free("y", 0, u + 1, 1 - ku % 2)
                pe.wait_ge(sum_done, u + 1)
                for j in range(JP):
                    m = pe.transpose(ring[:, y_bank(ku % 2), pairs[j]], x2t[:, ku % X2, pairs[j]], ident)
                m.then_inc(y_turned, 1)

            def pack(s, w):
                ring_free("pack", w, s * 2 + 1, 1)
                pe.wait_ge(pick_step, (s + 1) * PICK_OPS + PICK_OPS)
                for q in range(2):
                    t0 = w * UNIT_J + 4 * q
                    m = pe.transpose(ring[:, pack_bank(w), pairs[q]],
                                     pk[:, t0:t0 + 4, :, :, :].bitcast(F32).rearrange("p j g z e -> p (j g z e)"), ident)
                m.then_inc(pack_turned, 1)

            def slot(u, ku):
                if has(u + 3):
                    back(u + 3, ku + 3)
                if has(u):
                    bcast(2, u, ku)
                    bcast(3, u, ku)
                if has(u + 4):
                    turns(u + 4, ku + 4)
                if has(u):
                    bias(u, ku)
                    expert(0, u, ku)
                    bcast(4, u, ku)
                    bcast(5, u, ku)
                    expert(1, u, ku)
                    bcast(6, u, ku)
                    bcast(7, u, ku)
                if has(u + 4):
                    out_gate(u + 4)
                if has(u - 1):
                    y_turn(u - 1, ku - 1)
                if has(u):
                    expert(2, u, ku)
                if ku % 2 == 1 and has(u + 1):
                    pack((u - 1) // 2, 0)
                    pack((u - 1) // 2, 1)
                if has(u):
                    expert(3, u, ku)
                if has(u + 1):
                    bcast(0, u + 1, ku + 1)
                    bcast(1, u + 1, ku + 1)

            for u in range(-4, 2 * HEAD):
                slot(u, u)
            with pe.Fori(0, LOOPS) as i:
                for k in range(2 * HEAD, 2 * (HEAD + CYCLE)):
                    slot(i * (2 * CYCLE) + k, k)
            for u in range(2 * TAIL, UNITS + 1):
                slot(u, u)

        @block.vector
        def _(dve):
            stat_a = bst[:, :, :].rearrange("p r (q z) -> p r q z", q=Q)
            wide = lambda ap: ap[:, :].rearrange("p (r q) -> p r q", q=Q)
            by_chunk = lambda ap: ap.rearrange("p (s c) -> p s c", c=CHUNK)

            def bn(n, b, rows):
                for r in rows:
                    ins = dve.bn_stats(bst[:, r, :], xa[:, b, r, :].rearrange("p (q c) -> p c q", q=Q))
                if rows[-1] == ROWS - 1:
                    ins.then_inc(stat_step, 1)

            def rstd_a(n, ks):
                r_out = r_all[:, bass.ts(n, ROWS), :]
                for k in ks:
                    dve.wait_ge(stat_step, n * STAT_OPS_A + 1 + k)
                    if k == 0:
                        ins = dve.tensor_scalar(wide(nv), stat_a[:, :, :, 2], (1 + EPS_LN) / C, EPS_LN * EPS_OUTER,
                                                ALU.mult, ALU.add)
                    elif k == 1:
                        ins = dve.tensor_scalar(ny[:, :].bitcast(I32), nv[:, :].bitcast(I32), -0.5, SEED, ALU.mult, ALU.add)
                    elif k == 10:
                        ins = dve.scalar_tensor_tensor(r_out, wide(nt), 1.5, wide(ny), ALU.add, ALU.mult)
                    elif k == 11:
                        ins = dve.scalar_tensor_tensor(wide(nt), stat_a[:, :, :, 1], -1.0, r_out, ALU.mult, ALU.mult)
                    elif k == 12:
                        ins = dve.tensor_scalar(b_all[:, bass.ts(n, ROWS), :], wide(nt), 1.0, None, ALU.add)
                    elif k % 3 == 2:
                        ins = dve.tensor_tensor(nt[:, :], ny[:, :], ny[:, :], ALU.mult)
                    elif k % 3 == 0:
                        ins = dve.scalar_tensor_tensor(nt[:, :], nt[:, :], -0.5, nv[:, :], ALU.mult, ALU.mult)
                    else:
                        ins = dve.scalar_tensor_tensor(ny[:, :], nt[:, :], 1.5, ny[:, :], ALU.add, ALU.mult)
                    ins.then_inc(stats_ready if k == 12 else stat_step, 1)

            def wait_x(n, b):
                dve.wait_ge(x_in[b], n // 2 * 16 + 16 if isinstance(n, int) else (n - b) * 8 + 16)

            def left_right(n, row, b, before=lambda q: None):
                before(0)
                dve.wait_ge(sig_ready, n * ROWS + row + 1)
                if row == 0 and after(n, 2):
                    dve.wait_ge(stored[b], n // 2 * 16 if isinstance(n, int) else (n - b) * 8)
                for q in range(Q):
                    if q:
                        before(q)
                    ins = dve.scalar_tensor_tensor(
                        stage[:, b, q, :, row, :], by_chunk(pr_a[:, row % ROW_RING, q * LRG:q * LRG + 2 * C]),
                        mt[:, bass.ds(n * ROWS + row, 1), q], by_chunk(sig_a[:, row % ROW_RING, q, :]), ALU.mult, ALU.mult)
                ins.then_inc(lr_done, 1)

            def block_a(n, b, ahead=True):
                if ahead:
                    wait_x(n + 2, b)
                for row in range(ROWS):
                    def small(q):
                        k = (row - BN_ROWS) * Q + q
                        if ahead and 0 <= k < 13:
                            rstd_a(n + 2, (k,))

                    if ahead and row < BN_ROWS:
                        bn(n + 2, b, range(row * ROWS // BN_ROWS, (row + 1) * ROWS // BN_ROWS))
                    left_right(n, row, b, small)

            wait_x(0, 0)
            bn(0, 0, range(ROWS))
            rstd_a(0, range(13))

            in5, out1 = slice(0, 5 * C), slice(5 * C, 6 * C)
            dve.wait_ge(set_pe, 1)
            dve.tensor_scalar(w_proj[:, in5], ps_set[:, 0, in5], ln_col[:, 0:1], None, ALU.mult)
            dve.tensor_scalar(w_proj[:, out1], ps_set[:, 0, out1], ln_col[:, 2:3], None, ALU.mult).then_inc(set_step, 1)
            dve.wait_ge(set_step, 1)
            dve.scalar_tensor_tensor(w_diff[:, in5], ps_set[:, 0, in5], ln_col[:, 1:2], w_proj[:, in5], ALU.mult, ALU.subtract)
            dve.scalar_tensor_tensor(w_diff[:, out1], ps_set[:, 0, out1], ln_col[:, 3:4], w_proj[:, out1], ALU.mult, ALU.subtract)\
               .then_inc(set_dve, 1)
            wait_x(1, 1)
            bn(1, 1, range(ROWS))
            dve.wait_ge(pool_const, 5)
            dve.wait_ge(set_pe, 3)
            dve.tensor_tensor(w_proj[:, :], w_proj[:, :], ps_set[:, 4, 0:6 * C], ALU.add).then_inc(set_dve, 1)
            dve.wait_ge(set_dve, 2)
            dve.tensor_copy(w_hi[:, :], w_proj[:, 0:LRG]).then_inc(set_step, 1)
            dve.wait_ge(set_step, 2)
            dve.tensor_tensor(w_lo[:, :], w_proj[:, 0:LRG], w_hi[:, :].bitcast(F32), ALU.subtract).then_inc(set_dve, 1)
            for w in range(2):
                for half in range(2):
                    part = slice(half * C, half * C + C)
                    dve.tensor_copy(w_og[part, w, part], w_proj[part, (4 + w) * C:(5 + w) * C])
            dve.wait_ge(set_act, 1)

            rstd_a(1, range(13))
            block_a(0, 0)
            block_a(1, 1)
            with dve.Fori(1, BLOCKS // 2 - 1) as i:
                block_a(i * 2, 0)
                block_a(i * 2 + 1, 1)
            block_a(BLOCKS - 2, 0, False)
            block_a(BLOCKS - 1, 1, False)

            dve.wait_ge(set_pe, 4)
            for half in range(2):
                part = slice(half * C, half * C + C)
                dve.tensor_tensor(w_exp[part, :, :], e_nat[part, :, :].rearrange("p (e z) c -> p e z c", z=2)[:, :, half, :],
                                  ps_set[part, 6, :].rearrange("p (e z c) -> p e z c", e=EP, z=2)[:, :, half, :], ALU.subtract)
                dve.tensor_tensor(w_router[part, half * E:half * E + E], r_nat[part, :], ps_set[part, 7, 0:E], ALU.subtract)
            dve.tensor_copy(bias_hi[:, :, :], eb_wide[:, :, :]).then_inc(set_step, 1)
            dve.wait_ge(set_step, 3)
            dve.tensor_tensor(bias_lo[:, :, :], eb_wide[:, :, :], bias_hi[:, :, :].bitcast(F32), ALU.subtract).then_inc(set_dve, 1)

            with dve.Fori(0, CHUNKS) as c:
                for k in range(1, CHUNK, 2):
                    dve.wait_ge(ein_ready, c * CHUNK + k + 1)
                    dve.tensor_copy(t_all[:, bass.ds(c * CHUNK + k, 1), :].rearrange("p a n -> p (a n)"), ein[:, k % 4, :])\
                       .then_inc(ein_dve, 1)
            dve.wait_ge(ein_act, C // 2)
            dve.wait_ge(ein_dve, C // 2)

            def stats_t(s, k, js):
                for j in js:
                    ins = dve.bn_stats(bst_t[:, k % 2, j, :], t_all[:, :, bass.ds(s * STEP_J + 2 * j, 2)])
                if js[-1] == TOK // 2 - 1:
                    ins.then_inc(bn_t_done, 1)

            def rstd_c(s, k3, ks):
                b = k3 % 2
                t_stat = bst_t[:, b, :, :].rearrange("p j (t z) -> p j t z", t=2)
                x_stat = bst_x[:, b, :, :].rearrange("p j (t z) -> p j t z", t=2)
                pair = lambda ap: ap.rearrange("p (j t) -> p j t", t=2)
                for k in ks:
                    if k == 0:
                        if after(s, -1):
                            dve.wait_ge(back_done, s * 2 + 4)
                            dve.wait_ge(norm_ready, s * 2 + 4)
                            ins = dve.tensor_scalar(pair(v32[:, 0:TOK]), x_stat[:, :, :, 2], 1.0 / C, EPS_LN, ALU.mult, ALU.add)
                        else:
                            ins = dve.memset(v32[:, 0:TOK], 1.0)
                    elif k == 1:
                        if not isinstance(s, int) or s + 3 < STEPS:
                            dve.wait_ge(bn_t_done, s + 4)
                        ins = dve.tensor_scalar(pair(v32[:, TOK:2 * TOK]), t_stat[:, :, :, 2], 1.0 / C, EPS_LN, ALU.mult, ALU.add)
                    else:
                        dve.wait_ge(rstd_step, (s + 3) * (RSTD_OPS - 1) + k)
                        if k == 2:
                            ins = dve.tensor_scalar(y32[:, :].bitcast(I32), v32[:, :].bitcast(I32), -0.5, SEED, ALU.mult, ALU.add)
                        elif k == 11:
                            ins = dve.scalar_tensor_tensor(rr[:, b, :], t32[:, :], 1.5, y32[:, :], ALU.add, ALU.mult)
                        elif k == 12:
                            ins = dve.scalar_tensor_tensor(pair(t32[:, 0:TOK]), t_stat[:, :, :, 1], -1.0,
                                                           pair(rr[:, b, TOK:2 * TOK]), ALU.mult, ALU.mult)
                        elif k == 13:
                            ins = dve.tensor_scalar(bt[:, b, :], t32[:, 0:TOK], 1.0, None, ALU.add)
                        elif k % 3 == 0:
                            ins = dve.tensor_tensor(t32[:, :], y32[:, :], y32[:, :], ALU.mult)
                        elif k % 3 == 1:
                            ins = dve.scalar_tensor_tensor(t32[:, :], t32[:, :], -0.5, v32[:, :], ALU.mult, ALU.mult)
                        else:
                            ins = dve.scalar_tensor_tensor(y32[:, :], t32[:, :], 1.5, y32[:, :], ALU.add, ALU.mult)
                    ins.then_inc(rstd_ready if k == 13 else rstd_step, 1)

            per_tok = lambda ap: ap.unsqueeze(2).broadcast_to([P, TOK, E])
            per_expert = lambda ap: ap.unsqueeze(1).broadcast_to([P, TOK, E])

            def pick(s, k1, k3, ks):
                r2 = per_tok(rr[:, k3 % 2, 0:TOK])
                tt, ttr = dve.tensor_tensor, dve.tensor_reduce
                o1, o2 = oo[:, 0, :, :], oo[:, 1, :, :]
                for k in ks:
                    if k == 1:
                        dve.wait_ge(rstd_ready, s + 4)
                    else:
                        dve.wait_ge(pick_step, (s + 1) * PICK_OPS + k - 1)
                    if k == 1:
                        ins = tt(lo[:, :, :], lg[:, k1 % 2, :, :], r2, ALU.mult)
                    elif k == 2:
                        ins = tt(lo[:, :, :], lo[:, :, :], per_expert(router_bias[:, :]), ALU.add)
                    elif k == 3:
                        ins = ttr(m1[:, :], lo[:, :, :], AX.X, ALU.max)
                    elif k == 4:
                        ins = tt(o1, lo[:, :, :], per_tok(m1[:, :]), ALU.is_equal)
                    elif k == 5:
                        ins = tt(o1, o1, per_expert(order[:, :]), ALU.mult)
                    elif k == 6:
                        ins = ttr(pm[:, :], o1, AX.X, ALU.max)
                    elif k == 7:
                        ins = tt(o1, o1, per_tok(pm[:, :]), ALU.is_equal)
                    elif k == 8:
                        ins = dve.scalar_tensor_tensor(lo[:, :, :], o1, -BIG, lo[:, :, :], ALU.mult, ALU.add)
                    elif k == 9:
                        ins = ttr(m2[:, :], lo[:, :, :], AX.X, ALU.max)
                    elif k == 10:
                        ins = tt(dd[:, :], m1[:, :], m2[:, :], ALU.subtract)
                    elif k == 11:
                        ins = tt(o2, lo[:, :, :], per_tok(m2[:, :]), ALU.is_equal)
                    elif k == 12:
                        ins = tt(o2, o2, per_expert(order[:, :]), ALU.mult)
                    elif k == 13:
                        ins = ttr(pm[:, :], o2, AX.X, ALU.max)
                    elif k == 14:
                        ins = tt(o2, o2, per_tok(pm[:, :]), ALU.is_equal)
                    elif k == 15:
                        dve.wait_ge(soft_ready, s + 2)
                        ins = tt(oo[:, :, :, :], oo[:, :, :, :], ws[:, :, :].unsqueeze(3).broadcast_to([P, 2, TOK, E]), ALU.mult)
                    elif k == 16:
                        ins = tt(gg[:, :, 1, :], o1, o2, ALU.add)
                    elif k == 17:
                        ins = tt(gg[:, :, 0, :], gg[:, :, 1, :], r2, ALU.mult)
                    elif k == 18:
                        if after(s, 0):
                            dve.wait_ge(pack_turned, s * 2 + 2)
                        ins = dve.tensor_copy(pk[:, :, :, 0, :], gg[:, :, :, :])
                    else:
                        ins = tt(pk[:, :, :, 1, :], gg[:, :, :, :], pk[:, :, :, 0, :].bitcast(F32), ALU.subtract)
                    ins.then_inc(pick_step, 1)

            def scale(m, u, ku):
                dve.wait_ge(bcast_ready, u * TILES + m + 1)
                if m == 0:
                    dve.wait_ge(dup_ready, u + 1)
                if after(u, 1) or m >= NZ:
                    dve.wait_ge(expert_done, u * EP + m // 2 - 1)
                dve.tensor_tensor(zb[:, m % NZ, :], ring[:, bcast_bank(ku % 2, m), :], x2d[:, ku % 2, m % 2, :], ALU.mult)\
                   .then_inc(z_dve, 1)

            def total(u, ku):
                dve.wait_ge(expert_done, u * EP + EP)
                dve.tensor_tensor(x2t[:, ku % X2, :], b_m[:, :], x2t[:, ku % X2, :], ALU.add).then_inc(sum_done, 1)

            def gated(v):
                dve.wait_ge(gate_ready, v + 1)
                dve.wait_ge(og_ready, v + 1)
                dve.tensor_tensor(sig_c[:, :], b_t[:, :], sig_c[:, :], ALU.mult).then_inc(om_done, 1)

            def residual(v, kv):
                dve.wait_ge(om_done, v + 1)
                if after(v, X2):
                    dve.wait_ge(y_turned, v - X2 + 1)
                dve.tensor_tensor(x2t[:, kv % X2, :], b_x[:, :], sig_c[:, :], ALU.add).then_inc(x2_ready, 1)

            def back(w, kw, between=lambda n: None):
                dve.wait_ge(back_ready, w + 1)
                h, b = kw % 2, kw // 2 % 2
                for j in range(JP):
                    dve.bn_stats(bst_x[:, b, h * JP + j, :],
                                 b_d[:, j // 2, j % 2 * BACK:j % 2 * BACK + P].rearrange("p (t c) -> p c t", t=2))
                    between(j)
                logits = b_d[:, :, 0:2 * BACK].rearrange("p z (j n) -> p z j n", j=2)[:, :, :, P:BACK]
                dve.tensor_copy(lg[:, b, h * UNIT_J:(h + 1) * UNIT_J, :].rearrange("p (z j t) e -> p z j (t e)", z=2, j=2),
                                logits).then_inc(back_done, 1)

            def norm_x(v):
                dve.wait_ge(xc_in[v % XC], v // XC * 16 + 16)
                if v > 0:
                    dve.wait_ge(turns_ready, v)
                r_x, b_x1 = (ap[:, v * UNIT_J:(v + 1) * UNIT_J].unsqueeze(2).broadcast_to([P, UNIT_J, C]) for ap in (rx, bx))
                dve.tensor_tensor(xn[:, :, :], xc[:, v % XC, :, :], r_x, ALU.mult).then_inc(x_norm, 1)
                dve.wait_ge(x_norm, 2 * v + 1)
                dve.tensor_tensor(xn[:, :, :], xn[:, :, :], b_x1, ALU.add).then_inc(x_norm, 1)

            def slot(u, ku):
                h, v = ku % 2, u + 4
                s, k = (u - h) // 2, (ku - h) // 2
                step_rstd = not isinstance(s, int) or s + 1 < STEPS
                step_pick = not isinstance(s, int) or -1 <= s < STEPS - 1
                stats = not isinstance(s, int) or s + 4 < STEPS

                def rstd(*ks):
                    if step_rstd and h == 0:
                        rstd_c(s, k + 3, ks)

                def route(even, odd):
                    if step_pick:
                        pick(s, k + 1, k + 3, odd if h else even)

                def bn(even, odd):
                    js = odd if h else even
                    if stats and js:
                        stats_t(s + 4, k + 4, js)

                def between(n):
                    route((), (7 + n,))
                    if h and n == 1 and has(u):
                        scale(2, u, ku)

                if isinstance(u, int) and 0 < u + 5 < NX:
                    norm_x(u + 5)
                if has(u - 1):
                    total(u - 1, ku - 1)
                route((), (6,))
                if has(u + 3):
                    back(u + 3, ku + 3, between)
                else:
                    for n in range(JP):
                        between(n)
                early = isinstance(u, int) and u in (-3, -2)
                if early and has(v):
                    gated(v)
                    residual(v, ku + 4)
                rstd(0, 1, 2)
                route((), (11,))
                if has(u) and h:
                    scale(4, u, ku)
                if has(u) and h == 0:
                    scale(2, u, ku)
                rstd(3)
                route((), (12,))
                bn((0,), ())
                rstd(4)
                route((), (13,))
                bn((1,), ())
                rstd(5)
                route((), (14,))
                if has(u) and h == 0:
                    scale(4, u, ku)
                rstd(6)
                bn((2,), ())
                rstd(7)
                route((), (15,))
                if has(u):
                    scale(6, u, ku)
                rstd(8)
                bn((3,), ())
                rstd(9)
                route((), (16,))
                if has(u) and h == 0:
                    scale(7, u, ku)
                rstd(10)
                bn((4,), ())
                rstd(11)
                route((), (17,))
                bn((5,), ())
                rstd(12)
                route((), (18, 19))
                rstd(13)
                if has(v) and not early:
                    gated(v)
                route((1,), ())
                if has(v) and not early:
                    residual(v, ku + 4)
                route((2, 3), ())
                bn((), (6, 7))
                if has(u + 1):
                    scale(0, u + 1, ku + 1)
                route((4, 5), ())

            stats_t(0, 0, range(8))
            rstd_c(-3, 0, range(RSTD_OPS))
            norm_x(0)
            stats_t(1, 1, range(8))
            for u in range(-4, 2 * HEAD):
                slot(u, u)
            with dve.Fori(0, LOOPS) as i:
                for k in range(2 * HEAD, 2 * (HEAD + CYCLE)):
                    slot(i * (2 * CYCLE) + k, k)
            for u in range(2 * TAIL, UNITS + 1):
                slot(u, u)


_CONV = ["ln_in_w", "ln_in_b", "ln_c_w", "ln_c_b"] + [p + s for p in PROJ for s in ("_w", "_b")]


def kernel(**inputs):
    import numpy as _np
    import concourse.bacc as _bacc
    from concourse.bass_utils import run_bass_kernel_spmd as _run

    nc = _bacc.Bacc("TRN2", target_bir_lowering=False, num_devices=1)
    arrays, aps = {}, {}
    for name, value in inputs.items():
        a = _np.ascontiguousarray(value)
        arrays[f"in_{name}"] = a
        aps[name] = nc.dram_tensor(f"in_{name}", a.shape, mybir.dt.from_np(a.dtype), kind="ExternalInput").ap()
    out = nc.dram_tensor("out_0", (1, N, N, C), F32, kind="ExternalOutput").ap()
    metaformer_kernel(nc, aps["x"], aps["L0_conv_mask"], {n: aps["L0_conv_" + n] for n in _CONV},
                      aps["L0_ffn_router_w"], aps["L0_ffn_router_b"], aps["L0_ffn_expert_w"], aps["L0_ffn_expert_b"], out)
    return _run(nc, [arrays], core_ids=[0]).results[0]["out_0"]
```
